# Optimizing a Trainium2 kernel written in Bass

```python
import numpy as np
import jax
import jax.numpy as jnp

def _softmax(x, axis=-1):
    return jax.nn.softmax(x, axis=axis)

def _gelu(x):
    return jax.nn.gelu(x, approximate=True)

def _silu(x):
    return jax.nn.silu(x)

def _sigmoid(x):
    return jax.nn.sigmoid(x)

def _layernorm(x, axis=-1, eps=1e-05):
    m = jnp.mean(x, axis=axis, keepdims=True)
    v = jnp.var(x, axis=axis, keepdims=True)
    return (x - m) / jnp.sqrt(v + eps)

def _scatter_add(tgt, idx, src, axis=0):
    return tgt.at[idx].add(src)

def _segment_sum(src, seg, n):
    return jax.ops.segment_sum(src, seg, n)
kernel_name = 'mk_gnn_resnorm_d1_gnn_r8_bd7f1d'

def setup_inputs(seed: int=0):
    np.random.seed(seed)
    _w = jnp.asarray

    def _rec_inputs():
        import jax
        import jax.numpy as jnp
        _gk = jax.random.key(seed)
        x = 7.22e-05 + 1 * jax.random.normal(jax.random.fold_in(_gk, 1), (6250, 256), jnp.float32)
        src = jax.random.randint(jax.random.fold_in(_gk, 2), (100000,), 0, 6250, jnp.int32)
        dst = jnp.minimum((6250 * jax.random.uniform(jax.random.fold_in(_gk, 3), (100000,)) ** 2.0).astype(jnp.int32), 49999)
        _o = jnp.argsort(dst, stable=True)
        src = src[_o]
        dst = dst[_o]
        edge_attr_5 = jax.random.uniform(jax.random.fold_in(_gk, 11), (100000, 5), jnp.float32, 0.0, 99.9996)
        node_type_19 = jax.random.randint(jax.random.fold_in(_gk, 13), (6250,), 0, 19, jnp.int32)
        return (x, src, dst, edge_attr_5, node_type_19)
    x, src, dst, edge_attr_5, node_type_19 = _rec_inputs()

    def _L0_gnn_setup():
        import jax, jax.numpy as jnp
        import numpy as np
        N = 4096
        E = 16384
        IN = 256
        OUT = 256
        TD = 32
        H = 4
        T = 19
        PROJ = OUT - 2 * TD
        DK = (OUT - TD) // H
        SQRT_DK = float(np.sqrt(DK))
        LN_EPS = 1e-05

        def time_emb(t, w, b):
            return jnp.cos(jnp.log(t + 1.0)[:, None] * w[None, :] + b[None, :])

        def typed_linear(x, W, b, node_type):
            out = jnp.zeros((x.shape[0], W.shape[2]), x.dtype)
            for t in range(W.shape[0]):
                out = jnp.where((node_type == t)[:, None], x @ W[t] + b[t], out)
            return out

        def seg_softmax(att, idx, n):
            m = jax.ops.segment_max(att, idx, num_segments=n)
            e = jnp.exp(att - m[idx])
            s = jax.ops.segment_sum(e, idx, num_segments=n)
            return e / (s[idx] + 1e-16)
        key = jax.random.key(seed)
        ks = jax.random.split(key, 8)
        x = jax.random.normal(ks[0], (N, IN), jnp.float32)
        node_type = jax.random.randint(ks[1], (N,), 0, T, jnp.int32)
        edge_index = jax.random.randint(ks[2], (2, E), 0, N, jnp.int32)
        times = jax.random.uniform(ks[3], (E, 3), jnp.float32, 0.0, 100.0)
        edge_attr = jnp.concatenate([times, node_type[edge_index[0]][:, None].astype(jnp.float32), node_type[edge_index[1]][:, None].astype(jnp.float32)], axis=1)
        s = 0.02
        Wk = jax.random.normal(ks[4], (T, IN, PROJ), jnp.float32) * s
        Wq = jax.random.normal(ks[5], (T, IN, PROJ), jnp.float32) * s
        Wv = jax.random.normal(ks[6], (T, IN, PROJ), jnp.float32) * s
        bk = jnp.zeros((T, PROJ), jnp.float32)
        bq = jnp.zeros((T, PROJ), jnp.float32)
        bv = jnp.zeros((T, PROJ), jnp.float32)
        Wa = jax.random.normal(ks[7], (T, 2 * OUT, IN), jnp.float32) * s
        ba = jnp.zeros((T, IN), jnp.float32)
        gamma = jnp.ones((T, IN), jnp.float32)
        beta = jnp.zeros((T, IN), jnp.float32)
        w_time = jnp.asarray(1.0 / 10 ** np.linspace(0, 1.5, TD), jnp.float32)
        b_time = jnp.zeros((TD,), jnp.float32)
        return dict(x=x, node_type=node_type, edge_index=edge_index, edge_attr=edge_attr, Wk=Wk, bk=bk, Wq=Wq, bq=bq, Wv=Wv, bv=bv, Wa=Wa, ba=ba, gamma=gamma, beta=beta, w_time=w_time, b_time=b_time)
    _L0_gnn_all = _L0_gnn_setup()
    _L0_gnn_in = {k: v for k, v in _L0_gnn_all.items() if k in ('Wk', 'bk', 'Wq', 'bq', 'Wv', 'bv', 'Wa', 'ba', 'gamma', 'beta', 'w_time', 'b_time')}
    del _L0_gnn_all
    return {'x': x, 'src': src, 'dst': dst, 'edge_attr_5': edge_attr_5, 'node_type_19': node_type_19, 'L0_gnn_Wk': _L0_gnn_in['Wk'], 'L0_gnn_bk': _L0_gnn_in['bk'], 'L0_gnn_Wq': _L0_gnn_in['Wq'], 'L0_gnn_bq': _L0_gnn_in['bq'], 'L0_gnn_Wv': _L0_gnn_in['Wv'], 'L0_gnn_bv': _L0_gnn_in['bv'], 'L0_gnn_Wa': _L0_gnn_in['Wa'], 'L0_gnn_ba': _L0_gnn_in['ba'], 'L0_gnn_gamma': _L0_gnn_in['gamma'], 'L0_gnn_beta': _L0_gnn_in['beta'], 'L0_gnn_w_time': _L0_gnn_in['w_time'], 'L0_gnn_b_time': _L0_gnn_in['b_time']}

def reference(x, src, dst, edge_attr_5, node_type_19, L0_gnn_Wk, L0_gnn_bk, L0_gnn_Wq, L0_gnn_bq, L0_gnn_Wv, L0_gnn_bv, L0_gnn_Wa, L0_gnn_ba, L0_gnn_gamma, L0_gnn_beta, L0_gnn_w_time, L0_gnn_b_time):
    import jax
    import jax.numpy as jnp

    def _L0_gnn_ref(x, node_type, edge_index, edge_attr, Wk, bk, Wq, bq, Wv, bv, Wa, ba, gamma, beta, w_time, b_time):
        import jax, jax.numpy as jnp
        import numpy as np
        N = 4096
        E = 16384
        IN = 256
        OUT = 256
        TD = 32
        H = 4
        T = 19
        PROJ = OUT - 2 * TD
        DK = (OUT - TD) // H
        SQRT_DK = float(np.sqrt(DK))
        LN_EPS = 1e-05

        def time_emb(t, w, b):
            return jnp.cos(jnp.log(t + 1.0)[:, None] * w[None, :] + b[None, :])

        def typed_linear(x, W, b, node_type):
            out = jnp.zeros((x.shape[0], W.shape[2]), x.dtype)
            for t in range(W.shape[0]):
                out = jnp.where((node_type == t)[:, None], x @ W[t] + b[t], out)
            return out

        def seg_softmax(att, idx, n):
            m = jax.ops.segment_max(att, idx, num_segments=n)
            e = jnp.exp(att - m[idx])
            s = jax.ops.segment_sum(e, idx, num_segments=n)
            return e / (s[idx] + 1e-16)
        row, col = (edge_index[0], edge_index[1])
        n = x.shape[0]
        K = typed_linear(x, Wk, bk, node_type)
        Q = typed_linear(x, Wq, bq, node_type)
        V = typed_linear(x, Wv, bv, node_type)
        e0 = time_emb(edge_attr[:, 0], w_time, b_time)
        e1 = time_emb(edge_attr[:, 1], w_time, b_time)
        e2 = time_emb(edge_attr[:, 2], w_time, b_time)

        def edge_msgs(Kn, Qn, Vn, ek, eq):
            k = jnp.concatenate([Kn, ek], axis=1).reshape(-1, H, DK)
            q = jnp.concatenate([Qn, eq], axis=1).reshape(-1, H, DK)
            att = jnp.einsum('ehd,ed->eh', k, q.sum(axis=1)) / SQRT_DK
            v = jnp.concatenate([Vn, ek], axis=1).reshape(-1, H, DK)
            return (att, v)
        att, v = edge_msgs(K[row], Q[col], V[row], e1, e2)
        att_i, v_i = edge_msgs(K[col], Q[row], V[col], e2, e1)
        att = seg_softmax(att, col, n)
        att_i = seg_softmax(att_i, row, n)
        res = (v * att[:, :, None]).reshape(-1, H * DK)
        res = jnp.concatenate([res, e0], axis=1)
        res_i = (v_i * att_i[:, :, None]).reshape(-1, H * DK)
        res_i = jnp.concatenate([res_i, e0], axis=1)
        agg = jax.ops.segment_sum(res, col, num_segments=n) + jax.ops.segment_sum(res_i, row, num_segments=n)
        h = jnp.concatenate([agg, agg], axis=1)
        o = typed_linear(h, Wa, ba, node_type)
        y = o + x
        mu = y.mean(axis=-1, keepdims=True)
        var = y.var(axis=-1, keepdims=True)
        yn = (y - mu) / jnp.sqrt(var + LN_EPS)
        return yn * gamma[node_type] + beta[node_type]
    edge_index = jnp.stack([src, dst])
    x = _layernorm(x + _L0_gnn_ref(x, node_type_19, edge_index, edge_attr_5, L0_gnn_Wk, L0_gnn_bk, L0_gnn_Wq, L0_gnn_bq, L0_gnn_Wv, L0_gnn_bv, L0_gnn_Wa, L0_gnn_ba, L0_gnn_gamma, L0_gnn_beta, L0_gnn_w_time, L0_gnn_b_time), axis=-1)
    return x

_drawn_inputs = setup_inputs


def setup_inputs(seed=0):
    import zlib

    import numpy as np

    out = dict(_drawn_inputs(seed))
    spreads = {'L0_gnn_bk': (0.0, 0.8),
     'L0_gnn_bq': (0.0, 0.8),
     'L0_gnn_bv': (0.0, 0.8),
     'L0_gnn_ba': (0.0, 0.454),
     'L0_gnn_gamma': (1.0, 0.2),
     'L0_gnn_beta': (0.0, 0.1),
     'L0_gnn_b_time': (0.0, 0.1)}
    factors = {'L0_gnn_Wk': 8.0, 'L0_gnn_Wq': 8.0, 'L0_gnn_Wv': 5.708}
    for name, (base, spread) in spreads.items():
        noise = np.random.default_rng([zlib.crc32(name.encode()), seed]).standard_normal(out[name].shape)
        drawn = base * np.exp(spread * noise) if base else spread * noise
        out[name] = jnp.asarray(drawn.astype(out[name].dtype))
    for name, factor in factors.items():
        out[name] = (out[name] * factor).astype(out[name].dtype)
    return out
```

```python
from contextlib import ExitStack

import numpy as np

import concourse.bass as bass
from concourse import mybir

ALU = mybir.AluOpType
ACT = mybir.ActivationFunctionType
AX = mybir.AxisListType
F32 = mybir.dt.float32
BF16 = mybir.dt.bfloat16
I32 = mybir.dt.int32
U32 = mybir.dt.uint32

P = 128
HEADS = 4
TD = 32
BIG = float(2.0**100)
ROUND = 1.5 * 2.0**23
TWO_PI = 6.2831845
LN_EPS = 1e-5
UN = 4
CG = 8


def wait(eng, sem, value):
    if not (isinstance(value, int) and value <= 0):
        eng.wait_ge(sem, value)


def wait_apart(eng, mark, *waits):
    for s, v in waits:
        wait(eng, s, v)
    eng.sem_inc(mark, 1)


def at(base, n=1):
    return bass.ds(base, n)


def gnn_kernel(nc, x, src, dst, edge_attr, node_type, Wk, bk, Wq, bq, Wv, bv, Wa, ba, gamma, beta,
               w_time, b_time, out):
    N, D = x.shape
    E = src.shape[0]
    T, _, PROJ = Wk.shape
    DK = (PROJ + TD) // HEADS
    KW = HEADS * DK
    KQ = PROJ - 3 * DK
    SCALE = 1.0 / float(np.sqrt(DK))
    KC = D // P

    EP = max(p for p in range(1, P + 1) if E % p == 0)
    EC = E // EP
    NP_ = max(p for p in range(1, P + 1) if N % p == 0)
    NCOL = N // NP_
    NBLK = -(-N // P)
    BINS = 2 * NBLK
    ST = 2 * P
    NS = (2 * E + BINS * (ST - 1)) // ST
    NS = -(-NS // UN) * UN
    NT = (N + T * (P - 1)) // P
    NT += NT % 2
    NPAD = NBLK * P
    REC = 2 + 3 * TD
    HW = DK + 1
    RHS = HEADS * HW + TD
    NG = EC // CG
    assert EC % (2 * CG) == 0 and D == 2 * P and NS % UN == 0

    records = nc.dram_tensor("records", [NS * ST, REC], F32).ap()
    node_slots = nc.dram_tensor("node_slots", [NT * P, 2], I32).ap()
    kv_table = nc.dram_tensor("kv_table", [N, 2 * KW], F32).ap()
    q_table = nc.dram_tensor("q_table", [NPAD, DK], F32).ap()
    agg_table = nc.dram_tensor("agg_table", [NPAD, D], F32).ap()

    whole = ExitStack()
    early = ExitStack()

    def sem(name):
        return whole.enter_context(nc.semaphore(name))

    def keep(name, shape, dt):
        return whole.enter_context(nc.sbuf_tensor(name, shape, dt))

    def edge_keep(name, shape, dt):
        return early.enter_context(nc.sbuf_tensor(name, shape, dt))

    passed = [sem(f"passed{i}") for i in range(4)]

    iota_row = keep("iota_row", [P, P], F32)
    iota_col = keep("iota_col", [P, 1], F32)
    ident = keep("ident", [P, P], F32)
    ident_b = keep("ident_b", [P, P], BF16)
    big_ident = keep("big_ident", [P, P], BF16)
    ones = keep("ones", [P, P], F32)
    bin_of = keep("bin_of", [1, NS], I32)
    block_of = keep("block_of", [1, NS], I32)
    type_of = keep("type_of", [1, NT], I32)
    node_ids = keep("node_ids", [P, NT, 2], I32)

    meta = edge_keep("meta", [EP, EC, 2, 2], I32)
    slot = edge_keep("slot", [EP, 2, EC], I32)
    log_time = edge_keep("log_time", [EP, EC, 3], F32)

    def sort():
        ctx = ExitStack()

        def sb(name, shape, dt):
            return ctx.enter_context(nc.sbuf_tensor(name, shape, dt))

        def ps(name, shape):
            return ctx.enter_context(nc.psum_tensor(name, shape, F32))

        FR = 22
        FILLS = NS * ST // (P * FR)
        assert FILLS * P * FR == NS * ST
        ends = sb("ends", [EP, 2, EC], I32)
        high = sb("high", [EP, 2, EC], I32)
        key = sb("key", [EP, 2, EC], F32)
        flag = sb("flag", [EP, EC], F32)
        cum = sb("cum", [EP, EC], F32)
        pos = sb("pos", [EP, 2, EC], F32)
        times = sb("times", [EP, EC, 5], F32)
        ntype = sb("ntype", [NP_, NCOL], I32)
        nkey = sb("nkey", [NP_, NCOL], F32)
        nflag = sb("nflag", [NP_, NCOL], F32)
        ncum = sb("ncum", [NP_, NCOL], F32)
        npos = sb("npos", [NP_, NCOL], F32)
        nslot = sb("nslot", [NP_, NCOL], I32)
        nrec = sb("nrec", [NP_, NCOL, 2], I32)
        nfill = sb("nfill", [P, NT, 2], I32)
        fill = sb("fill", [P, FR, REC], F32)
        before = sb("before", [P, P], F32)
        iota_u = sb("iota_u", [P, NS], F32)
        counts = [sb("ecount", [P, BINS], F32), sb("ncount", [P, T], F32)]
        tiles_i = [sb("etiles_i", [P, BINS], I32), sb("ntiles_i", [P, T], I32)]
        tiles = [sb("etiles", [P, BINS], F32), sb("ntiles", [P, T], F32)]
        upto = [sb("eupto", [P, BINS], F32), sb("nupto", [P, T], F32)]
        first = [sb("efirst", [P, BINS], F32), sb("nfirst", [P, T], F32)]
        base = [sb("ebase", [P, BINS], F32), sb("nbase", [P, T], F32)]
        first_col = [sb("efirst_col", [P, 1], F32), sb("nfirst_col", [P, 1], F32)]
        begun = [sb("ebegun", [P, NS], F32), sb("nbegun", [P, NT], F32)]
        row = sb("row", [1, NS], F32)
        row2 = sb("row2", [1, NS], F32)

        off_ps = [ps("eoff_ps", [P, 512]), ps("noff_ps", [P, 512])]
        tot_ps = [ps("etot_ps", [P, 512]), ps("ntot_ps", [P, 512])]
        col_ps = ps("col_ps", [P, 512])
        map_ps = [ps("emap_ps", [P, 512]), ps("emap2_ps", [P, 512]), ps("nmap_ps", [P, 512])]
        half = NS // 2
        assert half <= 512

        ends_in, times_in, ntype_in = sem("ends_in"), sem("times_in"), sem("ntype_in")
        pool_done, fill_ready, filled = sem("pool_done"), sem("fill_ready"), sem("filled")
        nfilled, nslot_ready, nscattered = sem("nfilled"), sem("nslot_ready"), sem("nscattered")
        ids_in, dve_done, counted = sem("ids_in"), sem("dve_done"), sem("counted")
        summed, first_ready, cols_done = sem("summed"), sem("first_ready"), sem("cols_done")
        begun_ready, maps_done, logs = sem("begun_ready"), sem("maps_done"), sem("logs")

        with nc.Block() as block:
            @block.sync
            def _(sp):
                sp.dma_start(ends[:, 0, :], dst.rearrange("(p c) -> p c", p=EP)).then_inc(ends_in, 16)
                sp.dma_start(ends[:, 1, :], src.rearrange("(p c) -> p c", p=EP)).then_inc(ends_in, 16)
                sp.dma_start(ntype[:], node_type.rearrange("(p c) -> p c", p=NP_)).then_inc(ntype_in, 16)
                sp.dma_start(times[:], edge_attr.rearrange("(p c) k -> p c k", p=EP)).then_inc(times_in, 16)
                sp.wait_ge(fill_ready, 1)
                rec_rows = records.rearrange("(p n) r -> p n r", p=P)
                with sp.Fori(0, FILLS) as f:
                    sp.dma_start(rec_rows[:, at(f * FR, FR), :], fill[:]).then_inc(filled, 16)
                slots_by_p = node_slots.rearrange("(i p) c -> p i c", p=P)
                sp.dma_start(slots_by_p, nfill[:]).then_inc(nfilled, 16)
                sp.wait_ge(nscattered, 16 * NCOL)
                sp.dma_start(node_ids[:], slots_by_p).then_inc(ids_in, 16)
                sp.wait_ge(ids_in, 16)
                sp.wait_ge(filled, 16 * FILLS)

            @block.scalar
            def _(act):
                act.wait_ge(times_in, 16)
                nc.scalar.activation(log_time[:], times[:, :, 0:3], ACT.Ln, bias=1.0).then_inc(logs, 1)
                act.wait_ge(logs, 1)

            @block.gpsimd
            def _(pool):
                nc.gpsimd.iota(iota_row[:], [[1, P]], base=0, channel_multiplier=0,
                               allow_small_or_imprecise_dtypes=True).then_inc(pool_done, 1)
                nc.gpsimd.iota(iota_col[:], [[1, 1]], base=0, channel_multiplier=1,
                               allow_small_or_imprecise_dtypes=True).then_inc(pool_done, 1)
                nc.gpsimd.iota(iota_u[:], [[1, NS]], base=0, channel_multiplier=0,
                               allow_small_or_imprecise_dtypes=True).then_inc(pool_done, 1)
                nc.gpsimd.memset(ones[:], 1.0).then_inc(pool_done, 1)
                for c in range(2):
                    nc.gpsimd.iota(nrec[:, :, c], [[1, NCOL]], base=0,
                                   channel_multiplier=NCOL).then_inc(pool_done, 1)
                nc.gpsimd.iota(nfill[:, :, 0], [[0, NT]], base=N, channel_multiplier=1).then_inc(pool_done, 1)
                nc.gpsimd.memset(nfill[:, :, 1], 0).then_inc(pool_done, 1)
                nc.gpsimd.memset(fill[:], 0.0).then_inc(pool_done, 1)
                pool.wait_ge(pool_done, 9)
                nc.gpsimd.memset(fill[:, :, 0:1].bitcast(I32), P).then_inc(fill_ready, 1)
                pool.wait_ge(nslot_ready, 1)
                pool.wait_ge(nfilled, 16)
                for c in range(NCOL):
                    nc.gpsimd.indirect_dma_start(
                        node_slots, bass.IndirectOffsetOnAxis(nslot[:, c:c + 1], 0), nrec[:, c, :],
                        None).then_inc(nscattered, 16)

            @block.tensor
            def _(pe):
                pe.wait_ge(counted, 2)
                pe.wait_ge(dve_done, 1)
                for k, (rows, bins) in enumerate(((EP, BINS), (NP_, T))):
                    nc.tensor.matmul(off_ps[k][0:rows, 0:bins], before[0:rows, 0:rows],
                                     counts[k][0:rows, :], start=True, stop=True).then_inc(summed, 1)
                    nc.tensor.matmul(tot_ps[k][:, 0:bins], ones[0:rows, :], counts[k][0:rows, :],
                                     start=True, stop=True).then_inc(summed, 1)
                pe.wait_ge(first_ready, 2)
                for k, bins in enumerate((BINS, T)):
                    nc.tensor.matmul(col_ps[0:bins, k:k + 1], first[k][0:1, :], ones[0:1, 0:1],
                                     start=True, stop=True).then_inc(cols_done, 1)
                pe.wait_ge(begun_ready, 2)
                nc.tensor.matmul(map_ps[0][0:1, 0:half], ones[0:BINS, 0:1], begun[0][0:BINS, 0:half],
                                 start=True, stop=True)
                nc.tensor.matmul(map_ps[1][0:1, 0:half], ones[0:BINS, 0:1], begun[0][0:BINS, half:NS],
                                 start=True, stop=True)
                nc.tensor.matmul(map_ps[2][0:1, 0:NT], ones[0:T, 0:1], begun[1][0:T, :],
                                 start=True, stop=True).then_inc(maps_done, 1)

            @block.vector
            def _(dve):
                n = [0]

                def step(ins, sem_=dve_done):
                    n[0] += 1
                    ins.then_inc(sem_, 1)
                    dve.wait_ge(sem_, n[0])

                dve.wait_ge(pool_done, 9)
                step(nc.vector.tensor_scalar(before[:], iota_row[:], iota_col[:], None, ALU.is_gt))
                step(nc.vector.tensor_scalar(ident[:], iota_row[:], iota_col[:], None, ALU.is_equal))
                step(nc.vector.tensor_copy(ident_b[:], ident[:]))
                step(nc.vector.tensor_scalar(big_ident[:], ident[:], BIG, None, ALU.mult))

                dve.wait_ge(ntype_in, 16)
                step(nc.vector.tensor_copy(nkey[:], ntype[:]))
                dve.wait_ge(ends_in, 32)
                for d in range(2):
                    step(nc.vector.tensor_scalar(high[:, d, :], ends[:, d, :], 7, None,
                                                 ALU.arith_shift_right))
                    step(nc.vector.tensor_copy(key[:, d, :], high[:, d, :]))
                    step(nc.vector.tensor_scalar(meta[:, :, d, 0], ends[:, d, :], P - 1, None,
                                                 ALU.bitwise_and))
                    step(nc.vector.tensor_copy(meta[:, :, d, 1], ends[:, 1 - d, :]))

                sorts = [(key[:, 0, :], 0, 0, NBLK, flag, cum, pos[:, 0, :], EP),
                         (key[:, 1, :], 0, NBLK, NBLK, flag, cum, pos[:, 1, :], EP),
                         (nkey[:], 1, 0, T, nflag, ncum, npos[:], NP_)]
                for keys, k, b0, bins, fl, cu, po, rows in sorts:
                    with dve.Fori(0, bins) as b:
                        nc.vector.tensor_scalar(fl[:], keys, iota_row[0:rows, at(b)], None,
                                                ALU.is_equal).then_inc(dve_done, 1)
                        dve.wait_ge(dve_done, 2 * b + (n[0] + 1))
                        nc.vector.tensor_reduce(counts[k][0:rows, at(b + b0)], fl[:], AX.X,
                                                ALU.add).then_inc(dve_done, 1)
                        dve.wait_ge(dve_done, 2 * b + (n[0] + 2))
                    n[0] += 2 * bins
                nc.vector.memset(row[:], 0.0).then_inc(counted, 1)
                nc.vector.memset(row2[:], 0.0).then_inc(counted, 1)

                dve.wait_ge(summed, 4)
                for k, (bins, rows, log2) in enumerate(((BINS, EP, 8), (T, NP_, 7))):
                    step(nc.vector.tensor_scalar(tiles_i[k][:], tot_ps[k][:, 0:bins],
                                                 float(2**log2 - 1), None, ALU.add))
                    step(nc.vector.tensor_scalar(tiles_i[k][:], tiles_i[k][:], log2, None,
                                                 ALU.arith_shift_right))
                    step(nc.vector.tensor_copy(tiles[k][:], tiles_i[k][:]))
                    step(nc.vector.tensor_tensor_scan(upto[k][:], tiles[k][:], tiles[k][:], 0.0,
                                                      ALU.add, ALU.max))
                    step(nc.vector.tensor_tensor(first[k][:], upto[k][:], tiles[k][:], ALU.subtract))
                    step(nc.vector.scalar_tensor_tensor(
                        base[k][0:rows, :], first[k][0:rows, :], float(2**log2),
                        off_ps[k][0:rows, 0:bins], ALU.mult, ALU.add))
                nc.vector.memset(row[:], 0.0).then_inc(first_ready, 2)

                dve.wait_ge(cols_done, 2)
                for k, (bins, many) in enumerate(((BINS, NS), (T, NT))):
                    step(nc.vector.tensor_copy(first_col[k][0:bins, :], col_ps[0:bins, k:k + 1]))
                    step(nc.vector.tensor_scalar(begun[k][0:bins, :], iota_u[0:bins, 0:many],
                                                 first_col[k][0:bins, :], None, ALU.is_ge))
                nc.vector.memset(row2[:], 0.0).then_inc(begun_ready, 2)
                dve.wait_ge(maps_done, 1)
                dve.wait_ge(begun_ready, 2)
                dve.wait_ge(first_ready, 2)
                step(nc.vector.tensor_scalar(type_of[:], map_ps[2][0:1, 0:NT], -1.0, None, ALU.add))
                step(nc.vector.tensor_scalar(row[:, 0:half], map_ps[0][0:1, 0:half], -1.0, None, ALU.add))
                step(nc.vector.tensor_scalar(row[:, half:NS], map_ps[1][0:1, 0:half], -1.0, None, ALU.add))
                step(nc.vector.tensor_copy(bin_of[:], row[:]))
                step(nc.vector.tensor_scalar(row2[:], row[:], float(NBLK), -float(NBLK), ALU.is_ge,
                                             ALU.mult))
                step(nc.vector.tensor_tensor(block_of[:], row[:], row2[:], ALU.add))

                for keys, k, b0, bins, fl, cu, po, rows in reversed(sorts):
                    step(nc.vector.memset(po, 0.0))
                    with dve.Fori(0, bins) as b:
                        nc.vector.tensor_scalar(fl[:], keys, iota_row[0:rows, at(b)], None,
                                                ALU.is_equal).then_inc(dve_done, 1)
                        dve.wait_ge(dve_done, 3 * b + (n[0] + 1))
                        nc.vector.tensor_tensor_scan(cu[:], fl[:], fl[:], base[k][0:rows, at(b + b0)],
                                                     ALU.add, ALU.max).then_inc(dve_done, 1)
                        wait_apart(dve, passed[0], (dve_done, 3 * b + (n[0] + 2)))
                        nc.vector.copy_predicated(po, fl[:].bitcast(U32), cu[:]).then_inc(dve_done, 1)
                        dve.wait_ge(dve_done, 3 * b + (n[0] + 3))
                    n[0] += 3 * bins
                    if k == 1:
                        nc.vector.tensor_scalar(nslot[:], npos[:], -1.0, None,
                                                ALU.add).then_inc(nslot_ready, 1)
                step(nc.vector.tensor_scalar(slot[:], pos[:], -1.0, None, ALU.add))
        ctx.close()

    def nodes():
        ctx = ExitStack()

        def two(name, shape, dt):
            return [ctx.enter_context(nc.sbuf_tensor(f"{name}{h}", shape, dt)) for h in range(2)]

        def two_ps(name, shape):
            return [ctx.enter_context(nc.psum_tensor(f"{name}{h}", shape, F32)) for h in range(2)]

        xg = two("xg", [P, D], F32)
        xT = two("xT", [P, KC, P], F32)
        w = two("w", [P, KC, 3 * PROJ], F32)
        bias = two("bias", [1, 3 * PROJ], F32)
        kv = two("kv", [P, 2, KW], F32)
        q = two("q", [P, DK], F32)
        zeros = ctx.enter_context(nc.sbuf_tensor("zeros", [NPAD - N, DK], F32))
        tail_stored = sem("tail_stored")
        xT_ps = two_ps("xT_ps", [P, 512])
        kv_ps = two_ps("kv_ps", [P, 512])
        q_ps = two_ps("q_ps", [P, 512])

        w_in = [sem("w_in0"), sem("w_in1")]
        x_in = [sem("x_in0"), sem("x_in1")]
        stored = [sem("kv_stored0"), sem("kv_stored1")]
        gaps, turned, turned_sb = sem("gaps"), sem("turned"), sem("turned_sb")
        projected, kv_ready, q_sum, q_ready = sem("projected"), sem("kv_ready"), sem("q_sum"), sem("q_ready")

        def loop(eng, body):
            body(0)
            with eng.Fori(1, NT // 2) as it:
                body(it)

        with nc.Block() as block:
            @block.sync
            def _(sp):
                sp.wait_ge(gaps, 3)
                sp.dma_start(q_table[N:NPAD, :], zeros[:]).then_inc(tail_stored, 16)

                def body(it):
                    for h in range(2):
                        i = 2 * it + h
                        wait(sp, projected, i - 1)
                        t = sp.value_load(type_of[0:1, at(i)], min_val=0, max_val=T - 1)
                        for c, (W, b) in enumerate(((Wk, bk), (Wv, bv), (Wq, bq))):
                            sp.dma_start(w[h][:, :, c * PROJ:(c + 1) * PROJ],
                                         W[at(t)].rearrange("o (c k) n -> k (o c) n", k=P)
                                         ).then_inc(w_in[h], 16)
                            sp.dma_start(bias[h][:, c * PROJ:(c + 1) * PROJ],
                                         b[at(t), :]).then_inc(w_in[h], 16)
                loop(sp, body)
                sp.wait_ge(tail_stored, 16)

            @block.gpsimd
            def _(pool):
                for h in range(2):
                    nc.gpsimd.memset(kv[h][:], 0.0).then_inc(gaps, 1)
                nc.gpsimd.memset(zeros[:], 0.0).then_inc(gaps, 1)

                def gather(i):
                    wait(pool, turned, i - 1)
                    nc.gpsimd.indirect_dma_start(
                        xg[i % 2][:], None, x, bass.IndirectOffsetOnAxis(node_ids[:, i, 1:2], 0)
                    ).then_inc(x_in[i % 2], 16)

                gather(0)
                for i in range(NT):
                    if i + 1 < NT:
                        gather(i + 1)
                    pool.wait_ge(kv_ready, i + 1)
                    nc.gpsimd.indirect_dma_start(
                        kv_table, bass.IndirectOffsetOnAxis(node_ids[:, i, 0:1], 0),
                        kv[i % 2][:].rearrange("p c k -> p (c k)"), None,
                        bounds_check=N - 1, oob_is_err=False).then_inc(stored[i % 2], 16)
                    pool.wait_ge(q_ready, i + 1)
                    nc.gpsimd.indirect_dma_start(
                        q_table, bass.IndirectOffsetOnAxis(node_ids[:, i, 0:1], 0),
                        q[i % 2][:], None, bounds_check=N - 1, oob_is_err=False).then_inc(stored[i % 2], 16)
                for h in range(2):
                    pool.wait_ge(stored[h], 32 * (NT // 2))

            @block.tensor
            def _(pe):
                def body(it):
                    for h in range(2):
                        i = 2 * it + h
                        pe.wait_ge(x_in[h], 16 * it + 16)
                        wait(pe, turned_sb, i - 1)
                        for c in range(KC):
                            mm = nc.tensor.transpose(xT_ps[h][:, c * P:(c + 1) * P],
                                                     xg[h][:, c * P:(c + 1) * P], ident[:])
                        mm.then_inc(turned, 1)
                        pe.wait_ge(w_in[h], 96 * it + 96)
                        pe.wait_ge(turned_sb, i + 1)
                        wait(pe, kv_ready, i - 1)
                        wait(pe, q_ready, i - 1)
                        for ps, a, b in ((kv_ps[h], 0, 2 * PROJ), (q_ps[h], 2 * PROJ, 3 * PROJ)):
                            nc.tensor.matmul(ps[:, 0:b - a], ones[0:1, :], bias[h][:, a:b],
                                             start=True, stop=False)
                            for c in range(KC):
                                mm = nc.tensor.matmul(ps[:, 0:b - a], xT[h][:, c, :], w[h][:, c, a:b],
                                                      start=False, stop=(c == KC - 1))
                        mm.then_inc(projected, 1)
                loop(pe, body)

            @block.scalar
            def _(act):
                act.wait_ge(gaps, 3)

                def body(it):
                    for h in range(2):
                        i = 2 * it + h
                        act.wait_ge(turned, i + 1)
                        wait(act, projected, i - 1)
                        nc.scalar.copy(xT[h][:], xT_ps[h][:, 0:KC * P].rearrange("p (c k) -> p c k", c=KC)
                                       ).then_inc(turned_sb, 1)
                        act.wait_ge(projected, i + 1)
                        wait(act, stored[h], 32 * it)
                        nc.scalar.copy(kv[h][:, :, 0:PROJ],
                                       kv_ps[h][:, 0:2 * PROJ].rearrange("p (c k) -> p c k", c=2)
                                       ).then_inc(kv_ready, 1)
                loop(act, body)

            @block.vector
            def _(dve):
                def body(it):
                    for h in range(2):
                        i = 2 * it + h
                        dve.wait_ge(projected, i + 1)
                        wait(dve, stored[h], 32 * it)
                        nc.vector.tensor_reduce(
                            q[h][:], q_ps[h][:, 0:3 * DK].rearrange("p (h d) -> p d h", h=3),
                            AX.X, ALU.add).then_inc(q_sum, 1)
                        dve.wait_ge(q_sum, i + 1)
                        nc.vector.tensor_tensor(q[h][:, 0:KQ], q[h][:, 0:KQ], q_ps[h][:, 3 * DK:PROJ],
                                                ALU.add).then_inc(q_ready, 1)
                loop(dve, body)
        ctx.close()

    def edges():
        ctx = ExitStack()

        def sb(name, shape, dt):
            return ctx.enter_context(nc.sbuf_tensor(name, shape, dt))

        freq = sb("freq", [EP, 2, TD], F32)
        wb = sb("wb", [EP, 2, TD], F32)
        turns = [sb(f"turns{h}", [EP, CG, 3, TD], F32) for h in range(2)]
        whole_turns = [sb(f"whole_turns{h}", [EP, CG, 3, TD], F32) for h in range(2)]
        rec = [sb(f"rec{h}", [EP, CG, 2, REC], F32) for h in range(2)]
        idx = [sb(f"idx{h}", [EP, 2, CG], I32) for h in range(2)]
        wb_in, freq_ready, part = sem("wb_in"), sem("freq_ready"), sem("turns_part")
        turns_ready, meta_ready, emb_ready = sem("turns_ready"), sem("meta_ready"), sem("emb_ready")
        sent = [sem("sent0"), sem("sent1")]

        def loop(eng, body):
            body(0)
            with eng.Fori(1, NG // 2) as it:
                body(it)

        with nc.Block() as block:
            @block.sync
            def _(sp):
                sp.dma_start(wb[:, 0, :], w_time.partition_broadcast(EP)).then_inc(wb_in, 16)
                sp.dma_start(wb[:, 1, :], b_time.partition_broadcast(EP)).then_inc(wb_in, 16)

            @block.vector
            def _(dve):
                dve.wait_ge(wb_in, 32)
                nc.vector.tensor_scalar(freq[:, 0, :], wb[:, 0, :], float(1 / (2 * np.pi)), None,
                                        ALU.mult).then_inc(freq_ready, 1)
                nc.vector.tensor_scalar(freq[:, 1, :], wb[:, 1, :], float(1 / (2 * np.pi)), 0.25,
                                        ALU.mult, ALU.add).then_inc(freq_ready, 1)
                dve.wait_ge(freq_ready, 2)

                def body(it):
                    for h in range(2):
                        i = 2 * it + h
                        c0 = i * CG
                        shape = [EP, CG, 3, TD]
                        wait(dve, emb_ready, i - 1)
                        nc.vector.tensor_tensor(
                            turns[h][:], log_time[:, at(c0, CG), :].unsqueeze(3).broadcast_to(shape),
                            freq[:, 0:1, :].unsqueeze(1).broadcast_to(shape), ALU.mult).then_inc(part, 1)
                        dve.wait_ge(part, 3 * i + 1)
                        nc.vector.tensor_tensor(
                            turns[h][:], turns[h][:],
                            freq[:, 1:2, :].unsqueeze(1).broadcast_to(shape), ALU.add).then_inc(part, 1)
                        dve.wait_ge(part, 3 * i + 2)
                        nc.vector.tensor_scalar(whole_turns[h][:], turns[h][:], ROUND, -ROUND, ALU.add,
                                                ALU.add).then_inc(part, 1)
                        dve.wait_ge(part, 3 * i + 3)
                        nc.vector.tensor_tensor(turns[h][:], turns[h][:], whole_turns[h][:],
                                                ALU.subtract).then_inc(turns_ready, 1)
                        wait(dve, sent[h], 16 * 2 * CG * it)
                        nc.vector.tensor_copy(rec[h][:, :, :, 0:2].bitcast(I32),
                                              meta[:, at(c0, CG), :, :]).then_inc(meta_ready, 1)
                        nc.vector.tensor_copy(idx[h][:], slot[:, :, at(c0, CG)]).then_inc(meta_ready, 1)
                loop(dve, body)

            @block.scalar
            def _(act):
                def body(it):
                    for h in range(2):
                        i = 2 * it + h
                        act.wait_ge(turns_ready, i + 1)
                        wait(act, sent[h], 16 * 2 * CG * it)
                        emb = rec[h][:, :, :, 2:REC].rearrange("p c d (t w) -> p c d t w", w=TD)
                        nc.scalar.activation(emb[:, :, 0, :, :], turns[h][:], ACT.Sin, scale=TWO_PI)
                        for place, time in enumerate((0, 2, 1)):
                            ins = nc.scalar.activation(emb[:, :, 1, place, :], turns[h][:, :, time, :],
                                                       ACT.Sin, scale=TWO_PI)
                        ins.then_inc(emb_ready, 1)
                loop(act, body)

            @block.gpsimd
            def _(pool):
                def body(it):
                    for h in range(2):
                        i = 2 * it + h
                        wait_apart(pool, passed[1], (emb_ready, i + 1), (meta_ready, 2 * i + 2))
                        for c in range(CG):
                            for d in range(2):
                                nc.gpsimd.indirect_dma_start(
                                    records, bass.IndirectOffsetOnAxis(idx[h][:, d, c:c + 1], 0),
                                    rec[h][:, c, d, :], None).then_inc(sent[h], 16)
                loop(pool, body)
                for h in range(2):
                    pool.wait_ge(sent[h], 16 * 2 * CG * (NG // 2))
        ctx.close()

    def attention():
        ctx = ExitStack()

        def sb(name, shape, dt):
            return ctx.enter_context(nc.sbuf_tensor(name, shape, dt))

        def each(name, shape, dt, n=UN):
            return [sb(f"{name}{j}", shape, dt) for j in range(n)]

        acc = sb("acc", [P, BINS, RHS], F32)
        top = sb("top", [P, BINS, HEADS], F32)
        pick = sb("pick", [8, HEADS, P], BF16)
        pick_f = sb("pick_f", [8, HEADS], F32)
        inv = sb("inv", [P, BINS, HEADS], F32)

        rec = each("arec", [P, 2, REC], F32)
        qblk = each("qblk", [P, DK], F32)
        kv = each("akv", [P, 2, 2 * KW], F32)
        hot = each("hot", [P, 2, P], F32)
        hotT = each("hotT", [P, 2, P], F32)
        off = each("off", [P, 2, P], BF16)
        qs = each("qs", [P, 2, DK], F32)
        prod = each("prod", [P, 2, KW], F32, 2)
        score = each("score", [P, 2, HEADS], F32)
        parts = each("parts", [P, 2, 2, HEADS], BF16)
        partsT = each("partsT", [8, 2, P], BF16)
        tmax = each("tmax", [P, HEADS], F32)
        newtop = each("newtop", [P, HEADS], F32)
        drop = each("drop", [P, HEADS], F32)
        keepf = each("keepf", [P, HEADS], F32)
        below = each("below", [P, 2, HEADS], F32)
        rhs = each("rhs", [P, 2, RHS], F32)

        def bank(name, shape):
            return ctx.enter_context(nc.psum_tensor(name, shape, F32))

        hotT_ps = bank("hotT_ps", [P, 4, P])[:, 0:2, :]
        q_ps = bank("q_ps", [P, 512])[:, 0:2 * DK].rearrange("p (t d) -> p t d", t=2)
        top_ps = bank("top_ps", [P, 512])[:, 0:2 * HEADS].rearrange("p (t h) -> p t h", t=2)
        partsT_ps = bank("partsT_ps", [P, 4, P])[0:8, 0:2, :]
        wide = bank("wide", [P, HEADS, 2, P])
        sums_ps = [bank(f"sums_ps{b}", [P, 512])[:, 0:RHS] for b in range(2)]

        rec_in = [sem(f"rec_in{j}") for j in range(UN)]
        q_in = [sem(f"q_in{j}") for j in range(UN)]
        kv_in = [sem(f"kv_in{j}") for j in range(UN)]
        ready = sem("acc_ready")
        names = ("hot_done hotT_mm hotT_sb q_mm q_sb q_time ek_put e0_put prod_done score_done hi_done "
                 "lo_done parts_mm parts_sb bcast_mm tmax_done newtop_done drop_done top_kept top_mm "
                 "keepf_done below_done w_done wv_done sums_mm scaled acc_done")
        S = {n: sem(n) for n in names.split()}

        def four(v):
            return v.rearrange("p t (h d) -> p t h d", h=HEADS)

        def loop(eng, order):
            lags = [lag for _, lag in order]

            def turn(it, js, check):
                for j in js:
                    for stage, lag in order:
                        it2, j2 = shifted(it, j, lag)
                        if not check or 0 <= it2 < NS // UN:
                            stage(it2, j2, UN * it2 + j2)

            lead = max(0, max(lags))
            first = -(-lead // UN)
            turn(-first, range(UN - lead % UN if lead % UN else 0, UN), True)
            for it in range(1 - first, 2):
                turn(it, range(UN), True)
            with eng.Fori(2, NS // UN - 1) as it:
                turn(it, range(UN), False)
            for it in range(NS // UN - 1, NS // UN + 1):
                turn(it, range(UN), True)

        def shifted(it, j, d):
            k = j + d
            return it + k // UN, k % UN

        with nc.Block() as block:
            @block.sync
            def _(sp):
                def load(it, j, k):
                    wait(sp, S["sums_mm"], k - 3)
                    wait(sp, S["q_mm"], k - 3)
                    b = sp.value_load(block_of[0:1, at(k)], min_val=0, max_val=NBLK - 1)
                    sp.dma_start(rec[j][:], records[at(k * ST, ST), :].rearrange("(p t) r -> p t r", t=2)
                                 ).then_inc(rec_in[j], 16)
                    sp.dma_start(qblk[j][:], q_table[at(b * P, P), :]).then_inc(q_in[j], 16)
                loop(sp, [(load, 0)])

            @block.gpsimd
            def _(pool):
                nc.gpsimd.memset(acc[:], 0.0).then_inc(ready, 1)
                nc.gpsimd.memset(top[:], -BIG).then_inc(ready, 1)

                def gather(it, j, k):
                    wait_apart(pool, passed[2], (rec_in[j], 16 * it + 16), (S["wv_done"], k - 3))
                    for t in range(2):
                        nc.gpsimd.indirect_dma_start(
                            kv[j][:, t, :], None, kv_table,
                            bass.IndirectOffsetOnAxis(rec[j][:, t, 1:2].bitcast(I32), 0)
                        ).then_inc(kv_in[j], 16)
                loop(pool, [(gather, 0)])

            @block.tensor
            def _(pe):
                def turn_hot(it, j, k):
                    pe.wait_ge(S["hot_done"], k + 1)
                    wait(pe, S["hotT_sb"], 2 * k)
                    for t in range(2):
                        mm = nc.tensor.transpose(hotT_ps[:, t, :], hot[j][:, t, :], ident[:])
                    mm.then_inc(S["hotT_mm"], 1)

                def queries(it, j, k):
                    pe.wait_ge(S["hotT_sb"], 2 * k + 2)
                    pe.wait_ge(q_in[j], 16 * it + 16)
                    wait(pe, S["q_sb"], k)
                    for t in range(2):
                        mm = nc.tensor.matmul(q_ps[:, t, :], hotT[j][:, t, :], qblk[j][:],
                                              start=True, stop=True)
                    mm.then_inc(S["q_mm"], 1)

                def turn_parts(it, j, k):
                    pe.wait_ge(S["lo_done"], k + 1)
                    wait(pe, S["parts_sb"], k)
                    for t in range(2):
                        mm = nc.tensor.matmul(partsT_ps[:, t, :],
                                              parts[j][:, t, :, :].rearrange("p a h -> p (a h)"),
                                              ident_b[:], start=True, stop=True)
                    mm.then_inc(S["parts_mm"], 1)

                def spread_scores(it, j, k):
                    pe.wait_ge(S["parts_sb"], k + 1)
                    wait(pe, S["tmax_done"], k)
                    for hp in range(HEADS // 2):
                        nc.tensor.matmul(wide[:, 2 * hp:2 * hp + 2, :, :], big_ident[:],
                                         off[j][:].unsqueeze(1).broadcast_to([P, 2, 2, P]),
                                         start=True, stop=False, skip_group_check=True)
                        for h in (2 * hp, 2 * hp + 1):
                            mm = nc.tensor.matmul(wide[:, h, :, :], pick[:, h, :], partsT[j][:],
                                                  start=False, stop=True, skip_group_check=True)
                    mm.then_inc(S["bcast_mm"], 1)

                def tops(it, j, k):
                    pe.wait_ge(S["newtop_done"], k + 1)
                    wait(pe, S["below_done"], k)
                    for t in range(2):
                        mm = nc.tensor.matmul(top_ps[:, t, :], hotT[j][:, t, :], newtop[j][:],
                                              start=True, stop=True)
                    mm.then_inc(S["top_mm"], 1)

                def sums(it, j, k):
                    pe.wait_ge(S["wv_done"], k + 1)
                    pe.wait_ge(S["e0_put"], k + 1)
                    wait(pe, S["acc_done"], k)
                    for t in range(2):
                        mm = nc.tensor.matmul(sums_ps[j % 2], hot[j][:, t, :], rhs[j][:, t, :],
                                              start=(t == 0), stop=(t == 1))
                    mm.then_inc(S["sums_mm"], 1)

                pe.wait_ge(ready, 3)
                loop(pe, [(tops, 0), (turn_hot, 2), (turn_parts, 1), (spread_scores, 1), (queries, 2),
                          (sums, 0)])

            @block.scalar
            def _(act):
                def copy_hotT(it, j, k):
                    act.wait_ge(S["hotT_mm"], k + 1)
                    wait(act, S["top_mm"], k - 3)
                    wait(act, S["bcast_mm"], k - 3)
                    nc.scalar.copy(hotT[j][:], hotT_ps).then_inc(S["hotT_sb"], 1)
                    nc.scalar.activation(off[j][:], hotT_ps, ACT.Copy, bias=-1.0
                                         ).then_inc(S["hotT_sb"], 1)

                def put_e0(it, j, k):
                    act.wait_ge(rec_in[j], 16 * it + 16)
                    wait(act, S["sums_mm"], k - 3)
                    nc.scalar.copy(rhs[j][:, :, RHS - TD:RHS], rec[j][:, :, 2:2 + TD]).then_inc(S["e0_put"], 1)

                def put_ek(it, j, k):
                    act.wait_ge(kv_in[j], 32 * it + 32)
                    for t in range(2):
                        ins = nc.scalar.copy(
                            kv[j][:, t, :].rearrange("p (c k) -> p c k", c=2)[:, :, PROJ:KW],
                            rec[j][:, t:t + 1, 2 + TD:2 + 2 * TD].broadcast_to([P, 2, TD]))
                    ins.then_inc(S["ek_put"], 1)

                def copy_q(it, j, k):
                    act.wait_ge(S["q_mm"], k + 1)
                    wait(act, S["prod_done"], k - 3)
                    nc.scalar.copy(qs[j][:], q_ps).then_inc(S["q_sb"], 1)

                def copy_parts(it, j, k):
                    act.wait_ge(S["parts_mm"], k + 1)
                    wait(act, S["bcast_mm"], k - 3)
                    nc.scalar.copy(partsT[j][:], partsT_ps).then_inc(S["parts_sb"], 1)

                def factor(it, j, k):
                    act.wait_ge(S["drop_done"], k + 1)
                    wait(act, S["scaled"], k - 3)
                    nc.scalar.activation(keepf[j][:], drop[j][:], ACT.Exp, scale=SCALE
                                         ).then_inc(S["keepf_done"], 1)

                def weights(it, j, k):
                    act.wait_ge(S["below_done"], k + 1)
                    w = rhs[j][:, :, 0:HEADS * HW].rearrange("p t (h d) -> p t h d", h=HEADS)[:, :, :, DK]
                    nc.scalar.activation(w, below[j][:], ACT.Exp, scale=SCALE).then_inc(S["w_done"], 1)

                loop(act, [(factor, 0), (copy_hotT, 2), (weights, 0), (copy_parts, 1), (put_e0, 2),
                           (copy_q, 2), (put_ek, 2)])

            @block.vector
            def _(dve):
                nc.vector.tensor_tensor(pick_f[:], ident[0:8, 0:HEADS], ident[0:8, HEADS:2 * HEADS],
                                        ALU.add).then_inc(S["acc_done"], 1)
                dve.wait_ge(S["acc_done"], 1)
                nc.vector.tensor_copy(pick[:], pick_f[:].unsqueeze(2).broadcast_to([8, HEADS, P])
                                      ).then_inc(ready, 1)
                dve.wait_ge(ready, 3)

                def one_hot(it, j, k):
                    dve.wait_ge(rec_in[j], 16 * it + 16)
                    wait(dve, S["sums_mm"], k - 3)
                    for t in range(2):
                        ins = nc.vector.tensor_scalar(hot[j][:, t, :], iota_row[:],
                                                      rec[j][:, t, 0:1].bitcast(I32), None, ALU.is_equal)
                    ins.then_inc(S["hot_done"], 1)

                def scores(it, j, k):
                    dve.wait_ge(S["q_sb"], k + 1)
                    nc.vector.tensor_tensor(qs[j][:, :, KQ:DK], qs[j][:, :, KQ:DK],
                                            rec[j][:, :, 2 + 2 * TD:REC], ALU.add).then_inc(S["q_time"], 1)
                    dve.wait_ge(S["q_time"], k + 1)
                    dve.wait_ge(S["ek_put"], k + 1)
                    nc.vector.tensor_tensor(four(prod[j % 2][:]), four(kv[j][:, :, 0:KW]),
                                            qs[j][:].unsqueeze(2).broadcast_to([P, 2, HEADS, DK]),
                                            ALU.mult).then_inc(S["prod_done"], 1)
                    dve.wait_ge(S["prod_done"], k + 1)
                    nc.vector.tensor_reduce(score[j][:], four(prod[j % 2][:]), AX.X, ALU.add
                                            ).then_inc(S["score_done"], 1)
                    dve.wait_ge(S["score_done"], k + 1)
                    wait(dve, S["parts_mm"], k - 3)
                    nc.vector.tensor_copy(parts[j][:, :, 0, :], score[j][:]).then_inc(S["hi_done"], 1)
                    dve.wait_ge(S["hi_done"], k + 1)
                    nc.vector.tensor_tensor(parts[j][:, :, 1, :], score[j][:], parts[j][:, :, 0, :],
                                            ALU.subtract).then_inc(S["lo_done"], 1)

                def maximum(it, j, k):
                    dve.wait_ge(S["bcast_mm"], k + 1)
                    nc.vector.tensor_reduce(tmax[j][:], wide[:].rearrange("p h t e -> p h (t e)"),
                                            AX.X, ALU.max).then_inc(S["tmax_done"], 1)
                    b = dve.value_load(bin_of[0:1, at(k)], min_val=0, max_val=BINS - 1)
                    dve.wait_ge(S["tmax_done"], k + 1)
                    wait(dve, S["top_kept"], k)
                    wait(dve, S["top_mm"], k - 3)
                    mine = top[:, at(b), :].rearrange("p o h -> p (o h)")
                    nc.vector.tensor_tensor(newtop[j][:], tmax[j][:], mine, ALU.max
                                            ).then_inc(S["newtop_done"], 1)
                    dve.wait_ge(S["newtop_done"], k + 1)
                    wait(dve, S["keepf_done"], k - 3)
                    nc.vector.tensor_tensor(drop[j][:], mine, newtop[j][:], ALU.subtract
                                            ).then_inc(S["drop_done"], 1)
                    dve.wait_ge(S["drop_done"], k + 1)
                    nc.vector.tensor_tensor(mine, newtop[j][:], newtop[j][:], ALU.max).then_inc(S["top_kept"], 1)

                def distance(it, j, k):
                    dve.wait_ge(S["top_mm"], k + 1)
                    wait(dve, S["w_done"], k - 3)
                    nc.vector.tensor_tensor(below[j][:], score[j][:], top_ps, ALU.subtract
                                            ).then_inc(S["below_done"], 1)

                def weigh(it, j, k):
                    dve.wait_ge(S["w_done"], k + 1)
                    r = rhs[j][:, :, 0:HEADS * HW].rearrange("p t (h d) -> p t h d", h=HEADS)
                    nc.vector.tensor_tensor(r[:, :, :, 0:DK], four(kv[j][:, :, KW:2 * KW]),
                                            r[:, :, :, DK:HW].broadcast_to([P, 2, HEADS, DK]),
                                            ALU.mult).then_inc(S["wv_done"], 1)

                def add(it, j, k):
                    b = dve.value_load(bin_of[0:1, at(k)], min_val=0, max_val=BINS - 1)
                    dve.wait_ge(S["keepf_done"], k + 1)
                    dve.wait_ge(S["acc_done"], k + 1)
                    mine = acc[:, at(b), 0:HEADS * HW].rearrange("p o (h d) -> p (o h) d", h=HEADS)
                    nc.vector.tensor_tensor(mine, mine, keepf[j][:].unsqueeze(2).broadcast_to([P, HEADS, HW]),
                                            ALU.mult).then_inc(S["scaled"], 1)
                    dve.wait_ge(S["scaled"], k + 1)
                    dve.wait_ge(S["sums_mm"], k + 1)
                    mine = acc[:, at(b), :].rearrange("p o n -> p (o n)")
                    nc.vector.tensor_tensor(mine, mine, sums_ps[j % 2], ALU.add).then_inc(S["acc_done"], 1)

                loop(dve, [(maximum, 0), (one_hot, 2), (distance, 0), (scores, 1), (weigh, 0), (add, -1)])

                dve.wait_ge(S["acc_done"], NS + 1)
                parts_ = acc[:, :, 0:HEADS * HW].rearrange("p b (h d) -> p b h d", h=HEADS)
                fin = S["scaled"]
                nc.vector.tensor_scalar(inv[:], parts_[:, :, :, DK], 1e-16, None, ALU.add).then_inc(fin, 1)
                dve.wait_ge(fin, NS + 1)
                nc.vector.reciprocal(inv[:], inv[:]).then_inc(fin, 1)
                dve.wait_ge(fin, NS + 2)
                nc.vector.tensor_tensor(parts_[:, :, :, 0:DK], parts_[:, :, :, 0:DK],
                                        inv[:].unsqueeze(3).broadcast_to([P, BINS, HEADS, DK]),
                                        ALU.mult).then_inc(fin, 1)
                dve.wait_ge(fin, NS + 3)
                nc.vector.tensor_tensor(acc[:, 0:NBLK, :], acc[:, 0:NBLK, :], acc[:, NBLK:BINS, :],
                                        ALU.add).then_inc(fin, 1)
        ctx_sem = sem("agg_stored")
        with nc.Block() as block:
            @block.sync
            def _(sp):
                agg_rows = agg_table[0:NBLK * P, :].rearrange("(b p) d -> p b d", p=P)
                sp.wait_ge(S["scaled"], NS + 4)
                for h in range(HEADS):
                    sp.dma_start(agg_rows[:, :, h * DK:(h + 1) * DK],
                                 acc[:, 0:NBLK, h * HW:h * HW + DK]).then_inc(ctx_sem, 16)
                sp.dma_start(agg_rows[:, :, KW:D], acc[:, 0:NBLK, HEADS * HW:RHS]).then_inc(ctx_sem, 16)
                sp.wait_ge(ctx_sem, 16 * (HEADS + 1))
        ctx.close()

    def output():
        ctx = ExitStack()

        def two(name, shape, dt):
            return [ctx.enter_context(nc.sbuf_tensor(f"{name}{h}", shape, dt)) for h in range(2)]

        def two_ps(name, shape):
            return [ctx.enter_context(nc.psum_tensor(f"{name}{h}", shape, F32)) for h in range(2)]

        agg = two("oagg", [P, D], F32)
        xg = two("oxg", [P, D], F32)
        aggT = two("aggT", [P, KC, P], F32)
        wa = two("wa", [P, 2 * KC, D], F32)
        rows = two("rows", [1, 3, D], F32)
        y = two("y", [P, D], F32)
        z = two("z", [P, D], F32)
        res = two("res", [P, D], F32)
        stats = two("stats", [P, 6], F32)
        moments = two("moments", [P, 2], F32)
        root = two("root", [P, 1], F32)
        eps = ctx.enter_context(nc.sbuf_tensor("eps", [P, 1], F32))
        aggT_ps = two_ps("aggT_ps", [P, 512])
        y_ps = two_ps("y_ps", [P, 512])
        gb_ps = two_ps("gb_ps", [P, 512])

        wa_in = [sem("wa_in0"), sem("wa_in1")]
        in_ = [sem("nodes_in0"), sem("nodes_in1")]
        stored = [sem("out_stored0"), sem("out_stored1")]
        turned, turned_sb, y_mm = sem("agg_turned"), sem("agg_turned_sb"), sem("y_mm")
        var_ready, root_ready, norm, res_ready = sem("var_ready"), sem("root_ready"), sem("norm"), sem("res_ready")
        eps_set = sem("eps_set")

        def loop(eng, body):
            body(0)
            with eng.Fori(1, NT // 2) as it:
                body(it)

        with nc.Block() as block:
            @block.sync
            def _(sp):
                def body(it):
                    for h in range(2):
                        i = 2 * it + h
                        wait(sp, y_mm, i - 1)
                        t = sp.value_load(type_of[0:1, at(i)], min_val=0, max_val=T - 1)
                        sp.dma_start(wa[h][:], Wa[at(t)].rearrange("o (c k) n -> k (o c) n", k=P)
                                     ).then_inc(wa_in[h], 16)
                        for c, b in enumerate((ba, gamma, beta)):
                            sp.dma_start(rows[h][:, c, :], b[at(t), :]).then_inc(wa_in[h], 16)
                loop(sp, body)

            @block.gpsimd
            def _(pool):
                nc.gpsimd.memset(eps[:], LN_EPS).then_inc(eps_set, 1)

                def gather(i):
                    wait(pool, res_ready, i - 1)
                    for tile_, table in ((agg, agg_table), (xg, x)):
                        nc.gpsimd.indirect_dma_start(
                            tile_[i % 2][:], None, table,
                            bass.IndirectOffsetOnAxis(node_ids[:, i, 1:2], 0)).then_inc(in_[i % 2], 16)

                gather(0)
                for i in range(NT):
                    if i + 1 < NT:
                        gather(i + 1)
                    pool.wait_ge(res_ready, i + 1)
                    nc.gpsimd.indirect_dma_start(
                        out, bass.IndirectOffsetOnAxis(node_ids[:, i, 0:1], 0), res[i % 2][:], None,
                        bounds_check=N - 1, oob_is_err=False).then_inc(stored[i % 2], 16)
                for h in range(2):
                    pool.wait_ge(stored[h], 16 * (NT // 2))

            @block.tensor
            def _(pe):
                def body(it):
                    for h in range(2):
                        i = 2 * it + h
                        pe.wait_ge(in_[h], 32 * it + 32)
                        wait(pe, turned_sb, i - 1)
                        for c in range(KC):
                            mm = nc.tensor.transpose(aggT_ps[h][:, c * P:(c + 1) * P],
                                                     agg[h][:, c * P:(c + 1) * P], ident[:])
                        mm.then_inc(turned, 1)
                        pe.wait_ge(wa_in[h], 64 * it + 64)
                        pe.wait_ge(turned_sb, i + 1)
                        wait(pe, res_ready, i - 1)
                        nc.tensor.matmul(gb_ps[h][:], ones[0:1, :],
                                         rows[h][:, 1:3, :].rearrange("p c n -> p (c n)"),
                                         start=True, stop=True)
                        nc.tensor.matmul(y_ps[h][:, 0:D], ones[0:1, :], rows[h][:, 0, :],
                                         start=True, stop=False)
                        for c in range(2 * KC):
                            mm = nc.tensor.matmul(y_ps[h][:, 0:D], aggT[h][:, c % KC, :], wa[h][:, c, :],
                                                  start=False, stop=(c == 2 * KC - 1))
                        mm.then_inc(y_mm, 1)
                loop(pe, body)

            @block.scalar
            def _(act):
                act.wait_ge(eps_set, 1)

                def body(it):
                    for h in range(2):
                        i = 2 * it + h
                        act.wait_ge(turned, i + 1)
                        wait(act, y_mm, i - 1)
                        nc.scalar.copy(aggT[h][:],
                                       aggT_ps[h][:, 0:KC * P].rearrange("p (c k) -> p c k", c=KC)
                                       ).then_inc(turned_sb, 1)
                        for n in range(2):
                            act.wait_ge(var_ready, 2 * i + n + 1)
                            nc.scalar.activation(root[h][:], moments[h][:, 1:2], ACT.Sqrt,
                                                 bias=eps[:]).then_inc(root_ready, 1)
                loop(act, body)

            @block.vector
            def _(dve):
                def body(it):
                    for h in range(2):
                        i = 2 * it + h
                        done = [0]

                        def step(ins):
                            done[0] += 1
                            ins.then_inc(norm, 1)
                            wait_apart(dve, passed[3], (norm, 9 * i + done[0]))

                        def normalised(a, into, n):
                            step(nc.vector.bn_stats(stats[h][:], a))
                            nc.vector.bn_aggr(moments[h][:], stats[h][:]).then_inc(var_ready, 1)
                            dve.wait_ge(root_ready, 2 * i + n + 1)
                            step(nc.vector.reciprocal(root[h][:], root[h][:]))
                            step(nc.vector.tensor_scalar(into, a, moments[h][:, 0:1], root[h][:, 0:1],
                                                         ALU.subtract, ALU.mult))

                        dve.wait_ge(y_mm, i + 1)
                        dve.wait_ge(in_[h], 32 * it + 32)
                        step(nc.vector.tensor_tensor(y[h][:], y_ps[h][:, 0:D], xg[h][:], ALU.add))
                        normalised(y[h][:], z[h][:], 0)
                        step(nc.vector.tensor_tensor(z[h][:], z[h][:], gb_ps[h][:, 0:D], ALU.mult))
                        step(nc.vector.tensor_tensor(z[h][:], z[h][:], gb_ps[h][:, D:2 * D], ALU.add))
                        step(nc.vector.tensor_tensor(y[h][:], z[h][:], xg[h][:], ALU.add))
                        step(nc.vector.bn_stats(stats[h][:], y[h][:]))
                        nc.vector.bn_aggr(moments[h][:], stats[h][:]).then_inc(var_ready, 1)
                        dve.wait_ge(root_ready, 2 * i + 2)
                        step(nc.vector.reciprocal(root[h][:], root[h][:]))
                        wait(dve, stored[h], 16 * it)
                        nc.vector.tensor_scalar(res[h][:], y[h][:], moments[h][:, 0:1], root[h][:, 0:1],
                                                ALU.subtract, ALU.mult).then_inc(res_ready, 1)
                        STEPS[0] = done[0]
                STEPS = [0]
                loop(dve, body)
        ctx.close()

    sort()
    nodes()
    edges()
    early.close()
    attention()
    output()
    whole.close()


_INS = ['x', 'src', 'dst', 'edge_attr_5', 'node_type_19', 'L0_gnn_Wk', 'L0_gnn_bk', 'L0_gnn_Wq', 'L0_gnn_bq',
        'L0_gnn_Wv', 'L0_gnn_bv', 'L0_gnn_Wa', 'L0_gnn_ba', 'L0_gnn_gamma', 'L0_gnn_beta', 'L0_gnn_w_time',
        'L0_gnn_b_time']


def kernel(**inputs):
    import numpy as _np
    import concourse.bacc as _bacc
    from concourse import mybir as _mybir
    from concourse.bass_utils import run_bass_kernel_spmd as _run

    nc = _bacc.Bacc("TRN2", target_bir_lowering=False, num_devices=1)
    arrays, args = {}, []
    for name in _INS:
        a = _np.ascontiguousarray(inputs[name])
        arrays[f"in_{name}_dram"] = a
        args.append(nc.dram_tensor(f"in_{name}_dram", a.shape, _mybir.dt.from_np(a.dtype), kind="ExternalInput").ap())
    shape = inputs['x'].shape
    args.append(nc.dram_tensor("out_0_dram", list(shape), _mybir.dt.float32, kind="ExternalOutput").ap())
    gnn_kernel(nc, *args)
    r = _run(nc, [arrays], core_ids=[0])
    return r.results[0]["out_0_dram"]
```

```python
from contextlib import ExitStack

import numpy as np

import concourse.bass as bass
from concourse import mybir

ALU = mybir.AluOpType
ACT = mybir.ActivationFunctionType
AX = mybir.AxisListType
F32 = mybir.dt.float32
BF16 = mybir.dt.bfloat16
I32 = mybir.dt.int32
U32 = mybir.dt.uint32

P = 128
HEADS = 4
TD = 32
BIG = float(2.0**100)
ROUND = 1.5 * 2.0**23
TWO_PI = 6.2831845
LN_EPS = 1e-5
BLK = P - 2 * HEADS
UN = 8
CG = 8


def wait(eng, sem, value):
    if not (isinstance(value, int) and value <= 0):
        eng.wait_ge(sem, value)


def wait_apart(eng, mark, *waits):
    for s, v in waits:
        wait(eng, s, v)
    eng.sem_inc(mark, 1)


def at(base, n=1):
    return bass.ds(base, n)


def gnn_kernel(nc, x, src, dst, edge_attr, node_type, Wk, bk, Wq, bq, Wv, bv, Wa, ba, gamma, beta,
               w_time, b_time, out):
    N, D = x.shape
    E = src.shape[0]
    T, _, PROJ = Wk.shape
    DK = (PROJ + TD) // HEADS
    KW = HEADS * DK
    KQ = PROJ - 3 * DK
    SCALE = 1.0 / float(np.sqrt(DK))
    KC = D // P

    EP = max(p for p in range(1, P + 1) if E % p == 0)
    EC = E // EP
    NP_ = max(p for p in range(1, P + 1) if N % p == 0)
    NCOL = N // NP_
    NBLK = -(-N // BLK)
    BINS = 2 * NBLK
    ST = 2 * P
    NS = (2 * E + BINS * (ST - 1)) // ST
    NS = -(-NS // UN) * UN
    NT = (N + T * (P - 1)) // P
    NT += NT % 2
    NPAD = NBLK * BLK
    assert NPAD - N <= P
    REC = 2 + 3 * TD
    HW = DK + 1
    RHS = HEADS * HW + TD
    NG = EC // CG
    assert EC % (2 * CG) == 0 and D == 2 * P and NS % UN == 0

    records = nc.dram_tensor("records", [2 * E + ST, REC], F32).ap()
    node_slots = nc.dram_tensor("node_slots", [NT * P, 2], I32).ap()
    kv_table = nc.dram_tensor("kv_table", [N, 2 * KW], F32).ap()
    q_table = nc.dram_tensor("q_table", [NPAD, 3 * DK], BF16).ap()
    agg_table = nc.dram_tensor("agg_table", [NPAD, D], F32).ap()

    whole = ExitStack()
    early = ExitStack()

    def sem(name):
        return whole.enter_context(nc.semaphore(name))

    def keep(name, shape, dt):
        return whole.enter_context(nc.sbuf_tensor(name, shape, dt))

    def edge_keep(name, shape, dt):
        return early.enter_context(nc.sbuf_tensor(name, shape, dt))

    passed = [sem(f"passed{i}") for i in range(4)]

    iota_row = keep("iota_row", [P, P], F32)
    iota_col = keep("iota_col", [P, 1], F32)
    ident = keep("ident", [P, P], F32)
    ident_b = keep("ident_b", [P, P], BF16)
    ones = keep("ones", [P, P], F32)
    bin_of = keep("bin_of", [1, NS], I32)
    window_of = keep("window_of", [1, NS], I32)
    less_start = keep("less_start", [P, NS], F32)
    carried = keep("carried", [P, NS], F32)
    block_of = keep("block_of", [1, NS], I32)
    type_of = keep("type_of", [1, NT], I32)
    node_ids = keep("node_ids", [P, NT, 2], I32)

    unsorted = keep("unsorted", [1, 1], I32)

    meta = edge_keep("meta", [EP, 2, EC, 2], I32)
    slot = edge_keep("slot", [EP, 2, EC], I32)
    log_time = edge_keep("log_time", [EP, EC, 3], F32)

    def sort():
        ctx = ExitStack()

        def sb(name, shape, dt):
            return ctx.enter_context(nc.sbuf_tensor(name, shape, dt))

        def ps(name, shape):
            return ctx.enter_context(nc.psum_tensor(name, shape, F32))

        ends = sb("ends", [EP, 2, EC], I32)
        key = sb("key", [EP, 2, EC], F32)
        flag = sb("flag", [EP, EC], F32)
        next_dst = sb("next_dst", [EP, 2], I32)
        falls = sb("falls", [EP, 1], F32)
        cum = sb("cum", [EP, EC], F32)
        pos = sb("pos", [EP, 2, EC], F32)
        times = sb("times", [EP, EC, 5], F32)
        ntype = sb("ntype", [NP_, NCOL], I32)
        nkey = sb("nkey", [NP_, NCOL], F32)
        nflag = sb("nflag", [NP_, NCOL], F32)
        ncum = sb("ncum", [NP_, NCOL], F32)
        npos = sb("npos", [NP_, NCOL], F32)
        nslot = sb("nslot", [NP_, NCOL], I32)
        nrec = sb("nrec", [NP_, NCOL, 2], I32)
        nfill = sb("nfill", [P, NT, 2], I32)
        fill = sb("fill", [P, ST // P, REC], F32)
        before = sb("before", [P, P], F32)
        iota_u = sb("iota_u", [P, NS], F32)
        counts = [sb("ecount", [P, BINS], F32), sb("ncount", [P, T], F32)]
        tiles_i = [sb("etiles_i", [P, BINS], I32), sb("ntiles_i", [P, T], I32)]
        tiles = [sb("etiles", [P, BINS], F32), sb("ntiles", [P, T], F32)]
        upto = [sb("eupto", [P, BINS], F32), sb("nupto", [P, T], F32)]
        first = [sb("efirst", [P, BINS], F32), sb("nfirst", [P, T], F32)]
        base = [sb("ebase", [P, BINS], F32), sb("nbase", [P, T], F32)]
        first_col = [sb("efirst_col", [P, 1], F32), sb("nfirst_col", [P, 1], F32)]
        begun = [sb("ebegun", [P, NS], F32), sb("nbegun", [P, NT], F32)]
        row = sb("row", [1, NS], F32)
        row2 = sb("row2", [1, NS], F32)
        edges_upto = sb("edges_upto", [P, BINS], F32)
        edges_before = sb("edges_before", [P, BINS], F32)
        shift = sb("shift", [1, 1 + BINS], F32)
        rise = sb("rise", [1, BINS], F32)
        rise_col = sb("rise_col", [P, 1], F32)
        total = sb("total", [P, BINS], F32)

        off_ps = [ps("eoff_ps", [P, 512]), ps("noff_ps", [P, 512])]
        tot_ps = [ps("etot_ps", [P, 512]), ps("ntot_ps", [P, 512])]
        col_ps = ps("col_ps", [P, 512])
        map_ps = [ps("emap_ps", [P, 512]), ps("emap2_ps", [P, 512]), ps("nmap_ps", [P, 512])]
        half = NS // 2
        assert half <= 512

        ends_in, times_in, ntype_in = sem("ends_in"), sem("times_in"), sem("ntype_in")
        pool_done, fill_ready, filled = sem("pool_done"), sem("fill_ready"), sem("filled")
        nfilled, nslot_ready, nscattered = sem("nfilled"), sem("nslot_ready"), sem("nscattered")
        ids_in, dve_done, counted = sem("ids_in"), sem("dve_done"), sem("counted")
        summed, first_ready, cols_done = sem("summed"), sem("first_ready"), sem("cols_done")
        map_read, slots_done = sem("map_read"), sem("slots_done")
        begun_ready, maps_done, logs = sem("begun_ready"), sem("maps_done"), sem("logs")

        with nc.Block() as block:
            @block.sync
            def _(sp):
                sp.dma_start(ends[:, 0, :], dst.rearrange("(p c) -> p c", p=EP)).then_inc(ends_in, 16)
                sp.dma_start(ends[:, 1, :], src.rearrange("(p c) -> p c", p=EP)).then_inc(ends_in, 16)
                sp.wait_ge(pool_done, 1)
                sp.dma_start(next_dst[0:EP - 1, :], dst.rearrange("(p c) -> p c", p=EP)[1:EP, 0:2]
                             ).then_inc(ends_in, 16)
                sp.dma_start(ntype[:], node_type.rearrange("(p c) -> p c", p=NP_)).then_inc(ntype_in, 16)
                sp.dma_start(times[:], edge_attr.rearrange("(p c) k -> p c k", p=EP)).then_inc(times_in, 16)
                sp.wait_ge(fill_ready, 1)
                sp.dma_start(records[2 * E:2 * E + ST, :].rearrange("(p n) r -> p n r", p=P), fill[:]
                             ).then_inc(filled, 16)
                slots_by_p = node_slots.rearrange("(i p) c -> p i c", p=P)
                sp.dma_start(slots_by_p, nfill[:]).then_inc(nfilled, 16)
                sp.wait_ge(nscattered, 16 * NCOL)
                sp.dma_start(node_ids[:], slots_by_p).then_inc(ids_in, 16)
                sp.wait_ge(ids_in, 16)
                sp.wait_ge(filled, 16)

            @block.scalar
            def _(act):
                act.wait_ge(times_in, 16)
                nc.scalar.activation(log_time[:], times[:, :, 0:3], ACT.Ln, bias=1.0).then_inc(logs, 1)
                act.wait_ge(logs, 1)

            @block.gpsimd
            def _(pool):
                nc.gpsimd.memset(next_dst[:], N).then_inc(pool_done, 1)
                nc.gpsimd.iota(iota_row[:], [[1, P]], base=0, channel_multiplier=0,
                               allow_small_or_imprecise_dtypes=True).then_inc(pool_done, 1)
                nc.gpsimd.iota(iota_col[:], [[1, 1]], base=0, channel_multiplier=1,
                               allow_small_or_imprecise_dtypes=True).then_inc(pool_done, 1)
                nc.gpsimd.iota(iota_u[:], [[1, NS]], base=0, channel_multiplier=0,
                               allow_small_or_imprecise_dtypes=True).then_inc(pool_done, 1)
                nc.gpsimd.memset(ones[:], 1.0).then_inc(pool_done, 1)
                for c in range(2):
                    nc.gpsimd.iota(nrec[:, :, c], [[1, NCOL]], base=0,
                                   channel_multiplier=NCOL).then_inc(pool_done, 1)
                nc.gpsimd.iota(nfill[:, :, 0], [[0, NT]], base=N, channel_multiplier=1).then_inc(pool_done, 1)
                nc.gpsimd.memset(nfill[:, :, 1], 0).then_inc(pool_done, 1)
                nc.gpsimd.memset(fill[:], 0.0).then_inc(pool_done, 1)
                pool.wait_ge(pool_done, 10)
                nc.gpsimd.memset(fill[:, :, 0:1].bitcast(I32), BINS * BLK).then_inc(fill_ready, 1)
                pool.wait_ge(nslot_ready, 1)
                pool.wait_ge(nfilled, 16)
                for c in range(NCOL):
                    nc.gpsimd.indirect_dma_start(
                        node_slots, bass.IndirectOffsetOnAxis(nslot[:, c:c + 1], 0), nrec[:, c, :],
                        None).then_inc(nscattered, 16)

            @block.tensor
            def _(pe):
                pe.wait_ge(counted, 2)
                pe.wait_ge(dve_done, 1)
                nc.tensor.matmul(tot_ps[1][0:1, P:P + 1], falls[:], ones[0:EP, 0:1],
                                 start=True, stop=True).then_inc(summed, 1)
                for k, (rows, bins) in enumerate(((EP, BINS), (NP_, T))):
                    nc.tensor.matmul(off_ps[k][0:rows, 0:bins], before[0:rows, 0:rows],
                                     counts[k][0:rows, :], start=True, stop=True).then_inc(summed, 1)
                    nc.tensor.matmul(tot_ps[k][:, 0:bins], ones[0:rows, :], counts[k][0:rows, :],
                                     start=True, stop=True).then_inc(summed, 1)
                pe.wait_ge(first_ready, 2)
                for k, bins in enumerate((BINS, T)):
                    nc.tensor.matmul(col_ps[0:bins, k:k + 1], first[k][0:1, :], ones[0:1, 0:1],
                                     start=True, stop=True).then_inc(cols_done, 1)
                nc.tensor.matmul(col_ps[0:BINS, 2:3], rise[:], ones[0:1, 0:1],
                                 start=True, stop=True).then_inc(cols_done, 1)
                pe.wait_ge(begun_ready, 2)
                nc.tensor.matmul(map_ps[0][:, 0:half], ones[0:BINS, :], begun[0][0:BINS, 0:half],
                                 start=True, stop=True)
                nc.tensor.matmul(map_ps[1][:, 0:half], ones[0:BINS, :], begun[0][0:BINS, half:NS],
                                 start=True, stop=True)
                nc.tensor.matmul(map_ps[2][0:1, 0:NT], ones[0:T, 0:1], begun[1][0:T, :],
                                 start=True, stop=True).then_inc(maps_done, 1)
                pe.wait_ge(map_read, 1)
                nc.tensor.matmul(map_ps[0][0:1, 0:half], rise_col[0:BINS, :], begun[0][0:BINS, 0:half],
                                 start=True, stop=True)
                nc.tensor.matmul(map_ps[1][0:1, 0:half], rise_col[0:BINS, :], begun[0][0:BINS, half:NS],
                                 start=True, stop=True).then_inc(maps_done, 1)

            @block.vector
            def _(dve):
                n = [0]

                def step(ins, sem_=dve_done):
                    n[0] += 1
                    ins.then_inc(sem_, 1)
                    dve.wait_ge(sem_, n[0])

                dve.wait_ge(pool_done, 10)
                step(nc.vector.tensor_scalar(before[:], iota_row[:], iota_col[:], None, ALU.is_gt))
                step(nc.vector.tensor_scalar(ident[:], iota_row[:], iota_col[:], None, ALU.is_equal))
                step(nc.vector.tensor_copy(ident_b[:], ident[:]))

                dve.wait_ge(ntype_in, 16)
                step(nc.vector.tensor_copy(nkey[:], ntype[:]))
                dve.wait_ge(ends_in, 48)
                for d in range(2):
                    step(nc.vector.tensor_scalar(key[:, d, :], ends[:, d, :], 1.0 / BLK,
                                                 0.5 / BLK - 0.5, ALU.mult, ALU.add))
                    step(nc.vector.tensor_scalar(key[:, d, :], key[:, d, :], ROUND, -ROUND, ALU.add,
                                                 ALU.add))
                    step(nc.vector.tensor_scalar(meta[:, d, :, 0], ends[:, d, :], float(d * NBLK * BLK),
                                                 None, ALU.add))
                    step(nc.vector.tensor_copy(meta[:, d, :, 1], ends[:, 1 - d, :]))

                step(nc.vector.tensor_tensor(flag[:, 0:EC - 1], ends[:, 0, 0:EC - 1], ends[:, 0, 1:EC],
                                             ALU.is_gt))
                step(nc.vector.tensor_tensor(flag[:, EC - 1:EC], ends[:, 0, EC - 1:EC], next_dst[:, 0:1],
                                             ALU.is_gt))
                step(nc.vector.tensor_reduce(falls[:], flag[:], AX.X, ALU.add))

                sorts = [(key[:, 0, :], 0, 0, NBLK, flag, cum, pos[:, 0, :], EP),
                         (key[:, 1, :], 0, NBLK, NBLK, flag, cum, pos[:, 1, :], EP),
                         (nkey[:], 1, 0, T, nflag, ncum, npos[:], NP_)]
                for keys, k, b0, bins, fl, cu, po, rows in sorts:
                    with dve.Fori(0, bins) as b:
                        nc.vector.tensor_scalar(fl[:], keys, iota_row[0:rows, at(b)], None,
                                                ALU.is_equal).then_inc(dve_done, 1)
                        dve.wait_ge(dve_done, 2 * b + (n[0] + 1))
                        nc.vector.tensor_reduce(counts[k][0:rows, at(b + b0)], fl[:], AX.X,
                                                ALU.add).then_inc(dve_done, 1)
                        dve.wait_ge(dve_done, 2 * b + (n[0] + 2))
                    n[0] += 2 * bins
                nc.vector.memset(row[:], 0.0).then_inc(counted, 1)
                nc.vector.memset(row2[:], 0.0).then_inc(counted, 1)

                dve.wait_ge(summed, 5)
                step(nc.vector.tensor_copy(unsorted[:], tot_ps[1][0:1, P:P + 1]))
                step(nc.vector.tensor_copy(total[:], tot_ps[0][:, 0:BINS]))
                step(nc.vector.tensor_tensor_scan(edges_upto[:], total[:], total[:], 0.0, ALU.add,
                                                  ALU.max))
                step(nc.vector.tensor_tensor(edges_before[:], edges_upto[:], total[:], ALU.subtract))
                for k, (bins, rows, log2) in enumerate(((BINS, EP, 8), (T, NP_, 7))):
                    step(nc.vector.tensor_scalar(tiles_i[k][:], tot_ps[k][:, 0:bins],
                                                 float(2**log2 - 1), None, ALU.add))
                    step(nc.vector.tensor_scalar(tiles_i[k][:], tiles_i[k][:], log2, None,
                                                 ALU.arith_shift_right))
                    step(nc.vector.tensor_copy(tiles[k][:], tiles_i[k][:]))
                    step(nc.vector.tensor_tensor_scan(upto[k][:], tiles[k][:], tiles[k][:], 0.0,
                                                      ALU.add, ALU.max))
                    step(nc.vector.tensor_tensor(first[k][:], upto[k][:], tiles[k][:], ALU.subtract))
                step(nc.vector.tensor_tensor(base[0][0:EP, :], edges_before[0:EP, :],
                                             off_ps[0][0:EP, 0:BINS], ALU.add))
                step(nc.vector.scalar_tensor_tensor(base[1][0:NP_, :], first[1][0:NP_, :], float(P),
                                                    off_ps[1][0:NP_, 0:T], ALU.mult, ALU.add))
                step(nc.vector.memset(shift[:], 0.0))
                step(nc.vector.scalar_tensor_tensor(shift[:, 1:1 + BINS], first[0][0:1, :], -float(ST),
                                                    edges_before[0:1, :], ALU.mult, ALU.add))
                step(nc.vector.tensor_tensor(rise[:], shift[:, 1:1 + BINS], shift[:, 0:BINS],
                                             ALU.subtract))
                nc.vector.memset(row[:], 0.0).then_inc(first_ready, 2)

                dve.wait_ge(cols_done, 3)
                step(nc.vector.tensor_copy(rise_col[0:BINS, :], col_ps[0:BINS, 2:3]))
                for k, (bins, many) in enumerate(((BINS, NS), (T, NT))):
                    step(nc.vector.tensor_copy(first_col[k][0:bins, :], col_ps[0:bins, k:k + 1]))
                    step(nc.vector.tensor_scalar(begun[k][0:bins, :], iota_u[0:bins, 0:many],
                                                 first_col[k][0:bins, :], None, ALU.is_ge))
                nc.vector.memset(row2[:], 0.0).then_inc(begun_ready, 2)
                dve.wait_ge(maps_done, 1)
                dve.wait_ge(begun_ready, 2)
                dve.wait_ge(first_ready, 2)
                step(nc.vector.tensor_scalar(type_of[:], map_ps[2][0:1, 0:NT], -1.0, None, ALU.add))
                step(nc.vector.tensor_scalar(row[:, 0:half], map_ps[0][0:1, 0:half], -1.0, None, ALU.add))
                step(nc.vector.tensor_scalar(row[:, half:NS], map_ps[1][0:1, 0:half], -1.0, None, ALU.add))
                for n2 in range(2):
                    step(nc.vector.tensor_scalar(less_start[:, n2 * half:(n2 + 1) * half],
                                                 map_ps[n2][:, 0:half], -1.0, -float(BLK), ALU.add,
                                                 ALU.mult))
                step(nc.vector.memset(carried[:], 0.0))
                step(nc.vector.tensor_tensor(carried[:, 1:NS], less_start[:, 1:NS],
                                             less_start[:, 0:NS - 1], ALU.is_equal))
                step(nc.vector.tensor_scalar(carried[:], carried[:], BIG * 2.0**20, -BIG, ALU.mult,
                                             ALU.add))
                nc.vector.memset(row2[:], 0.0).then_inc(map_read, 1)
                dve.wait_ge(map_read, 1)
                step(nc.vector.tensor_copy(bin_of[:], row[:]))
                step(nc.vector.tensor_scalar(row2[:], row[:], float(NBLK), -float(NBLK), ALU.is_ge,
                                             ALU.mult))
                step(nc.vector.tensor_tensor(block_of[:], row[:], row2[:], ALU.add))
                dve.wait_ge(maps_done, 2)
                for n2 in range(2):
                    part = slice(n2 * half, (n2 + 1) * half)
                    step(nc.vector.scalar_tensor_tensor(row[:, part], iota_u[0:1, part], float(ST),
                                                        map_ps[n2][0:1, 0:half], ALU.mult, ALU.add))
                step(nc.vector.tensor_scalar(window_of[:], row[:], float(2 * E), None, ALU.min))

                def rank(keys, k, b0, bins, fl, cu, po, rows, into, sem_):
                    step(nc.vector.memset(po, 0.0))
                    with dve.Fori(0, bins) as b:
                        nc.vector.tensor_scalar(fl[:], keys, iota_row[0:rows, at(b)], None,
                                                ALU.is_equal).then_inc(dve_done, 1)
                        dve.wait_ge(dve_done, 3 * b + (n[0] + 1))
                        nc.vector.tensor_tensor_scan(cu[:], fl[:], fl[:], base[k][0:rows, at(b + b0)],
                                                     ALU.add, ALU.max).then_inc(dve_done, 1)
                        wait_apart(dve, passed[0], (dve_done, 3 * b + (n[0] + 2)))
                        nc.vector.copy_predicated(po, fl[:].bitcast(U32), cu[:]).then_inc(dve_done, 1)
                        dve.wait_ge(dve_done, 3 * b + (n[0] + 3))
                    n[0] += 3 * bins
                    nc.vector.tensor_scalar(into, po, -1.0, None, ALU.add).then_inc(sem_, 1)

                rank(*sorts[2], nslot[:], nslot_ready)
                rank(*sorts[1], slot[:, 1, :], slots_done)
                step(nc.vector.memset(slot[:, 0, :], 0))
                falls_in = dve.value_load(unsorted[0:1, 0:1], min_val=0, max_val=E)
                with dve.If(falls_in > 0):
                    rank(*sorts[0], slot[:, 0, :], slots_done)
        ctx.close()

    def nodes():
        ctx = ExitStack()

        def two(name, shape, dt):
            return [ctx.enter_context(nc.sbuf_tensor(f"{name}{h}", shape, dt)) for h in range(2)]

        def two_ps(name, shape):
            return [ctx.enter_context(nc.psum_tensor(f"{name}{h}", shape, F32)) for h in range(2)]

        xg = two("xg", [P, D], F32)
        xT = two("xT", [P, KC, P], F32)
        w = two("w", [P, KC, 3 * PROJ], F32)
        bias = two("bias", [1, 3 * PROJ], F32)
        kv = two("kv", [P, 2, KW], F32)
        q = two("q", [P, DK], F32)
        q3 = two("q3", [P, 3, DK], BF16)
        zeros = ctx.enter_context(nc.sbuf_tensor("zeros", [NPAD - N, 3 * DK], BF16))
        tail_stored = sem("tail_stored")
        xT_ps = two_ps("xT_ps", [P, 512])
        kv_ps = two_ps("kv_ps", [P, 512])
        q_ps = two_ps("q_ps", [P, 512])

        w_in = [sem("w_in0"), sem("w_in1")]
        x_in = [sem("x_in0"), sem("x_in1")]
        stored = [sem("kv_stored0"), sem("kv_stored1")]
        gaps, turned, turned_sb = sem("gaps"), sem("turned"), sem("turned_sb")
        projected, kv_ready, q_sum, q_ready = sem("projected"), sem("kv_ready"), sem("q_sum"), sem("q_ready")

        def loop(eng, body):
            body(0)
            with eng.Fori(1, NT // 2) as it:
                body(it)

        with nc.Block() as block:
            @block.sync
            def _(sp):
                sp.wait_ge(gaps, 3)
                sp.dma_start(q_table[N:NPAD, :], zeros[:]).then_inc(tail_stored, 16)

                def body(it):
                    for h in range(2):
                        i = 2 * it + h
                        wait(sp, projected, i - 1)
                        t = sp.value_load(type_of[0:1, at(i)], min_val=0, max_val=T - 1)
                        for c, (W, b) in enumerate(((Wk, bk), (Wv, bv), (Wq, bq))):
                            sp.dma_start(w[h][:, :, c * PROJ:(c + 1) * PROJ],
                                         W[at(t)].rearrange("o (c k) n -> k (o c) n", k=P)
                                         ).then_inc(w_in[h], 16)
                            sp.dma_start(bias[h][:, c * PROJ:(c + 1) * PROJ],
                                         b[at(t), :]).then_inc(w_in[h], 16)
                loop(sp, body)
                sp.wait_ge(tail_stored, 16)

            @block.gpsimd
            def _(pool):
                for h in range(2):
                    nc.gpsimd.memset(kv[h][:], 0.0).then_inc(gaps, 1)
                nc.gpsimd.memset(zeros[:], 0.0).then_inc(gaps, 1)

                def gather(i):
                    wait(pool, turned, i - 1)
                    nc.gpsimd.indirect_dma_start(
                        xg[i % 2][:], None, x, bass.IndirectOffsetOnAxis(node_ids[:, i, 1:2], 0)
                    ).then_inc(x_in[i % 2], 16)

                gather(0)
                for i in range(NT):
                    if i + 1 < NT:
                        gather(i + 1)
                    pool.wait_ge(kv_ready, i + 1)
                    nc.gpsimd.indirect_dma_start(
                        kv_table, bass.IndirectOffsetOnAxis(node_ids[:, i, 0:1], 0),
                        kv[i % 2][:].rearrange("p c k -> p (c k)"), None,
                        bounds_check=N - 1, oob_is_err=False).then_inc(stored[i % 2], 16)
                    pool.wait_ge(q_ready, i + 1)
                    nc.gpsimd.indirect_dma_start(
                        q_table, bass.IndirectOffsetOnAxis(node_ids[:, i, 0:1], 0),
                        q3[i % 2][:].rearrange("p a d -> p (a d)"), None, bounds_check=N - 1, oob_is_err=False).then_inc(stored[i % 2], 16)
                for h in range(2):
                    pool.wait_ge(stored[h], 32 * (NT // 2))

            @block.tensor
            def _(pe):
                def body(it):
                    for h in range(2):
                        i = 2 * it + h
                        pe.wait_ge(x_in[h], 16 * it + 16)
                        wait(pe, turned_sb, i - 1)
                        for c in range(KC):
                            mm = nc.tensor.transpose(xT_ps[h][:, c * P:(c + 1) * P],
                                                     xg[h][:, c * P:(c + 1) * P], ident[:])
                        mm.then_inc(turned, 1)
                        pe.wait_ge(w_in[h], 96 * it + 96)
                        pe.wait_ge(turned_sb, i + 1)
                        wait(pe, kv_ready, i - 1)
                        wait(pe, q_ready, i - 1)
                        for ps, a, b in ((kv_ps[h], 0, 2 * PROJ), (q_ps[h], 2 * PROJ, 3 * PROJ)):
                            nc.tensor.matmul(ps[:, 0:b - a], ones[0:1, :], bias[h][:, a:b],
                                             start=True, stop=False)
                            for c in range(KC):
                                mm = nc.tensor.matmul(ps[:, 0:b - a], xT[h][:, c, :], w[h][:, c, a:b],
                                                      start=False, stop=(c == KC - 1))
                        mm.then_inc(projected, 1)
                loop(pe, body)

            @block.scalar
            def _(act):
                act.wait_ge(gaps, 3)

                def body(it):
                    for h in range(2):
                        i = 2 * it + h
                        act.wait_ge(turned, i + 1)
                        wait(act, projected, i - 1)
                        nc.scalar.copy(xT[h][:], xT_ps[h][:, 0:KC * P].rearrange("p (c k) -> p c k", c=KC)
                                       ).then_inc(turned_sb, 1)
                        act.wait_ge(projected, i + 1)
                        wait(act, stored[h], 32 * it)
                        nc.scalar.copy(kv[h][:, :, 0:PROJ],
                                       kv_ps[h][:, 0:2 * PROJ].rearrange("p (c k) -> p c k", c=2)
                                       ).then_inc(kv_ready, 1)
                loop(act, body)

            @block.vector
            def _(dve):
                def body(it):
                    for h in range(2):
                        i = 2 * it + h
                        dve.wait_ge(projected, i + 1)
                        nc.vector.tensor_reduce(
                            q[h][:], q_ps[h][:, 0:3 * DK].rearrange("p (h d) -> p d h", h=3),
                            AX.X, ALU.add).then_inc(q_sum, 1)
                        dve.wait_ge(q_sum, 5 * i + 1)
                        nc.vector.tensor_tensor(q[h][:, 0:KQ], q[h][:, 0:KQ], q_ps[h][:, 3 * DK:PROJ],
                                                ALU.add).then_inc(q_sum, 1)
                        dve.wait_ge(q_sum, 5 * i + 2)
                        wait(dve, stored[h], 32 * it)
                        nc.vector.tensor_tensor(q3[h][:, 0, :], q[h][:], q[h][:], ALU.max).then_inc(q_sum, 1)
                        dve.wait_ge(q_sum, 5 * i + 3)
                        nc.vector.tensor_tensor(q[h][:], q[h][:], q3[h][:, 0, :], ALU.subtract
                                                ).then_inc(q_sum, 1)
                        dve.wait_ge(q_sum, 5 * i + 4)
                        nc.vector.tensor_tensor(q3[h][:, 1, :], q[h][:], q[h][:], ALU.max).then_inc(q_sum, 1)
                        dve.wait_ge(q_sum, 5 * i + 5)
                        nc.vector.tensor_tensor(q3[h][:, 2, :], q[h][:], q3[h][:, 1, :], ALU.subtract
                                                ).then_inc(q_ready, 1)
                loop(dve, body)
        ctx.close()

    def edges():
        ctx = ExitStack()

        def sb(name, shape, dt):
            return ctx.enter_context(nc.sbuf_tensor(name, shape, dt))

        freq = sb("freq", [EP, 2, TD], F32)
        wb = sb("wb", [EP, 2, TD], F32)
        turns = [sb(f"turns{h}", [EP, CG, 3, TD], F32) for h in range(2)]
        whole_turns = [sb(f"whole_turns{h}", [EP, CG, 3, TD], F32) for h in range(2)]
        rec = [sb(f"rec{h}", [EP, 2, CG, REC], F32) for h in range(2)]
        idx = [sb(f"idx{h}", [EP, 2, CG], I32) for h in range(2)]
        wb_in, freq_ready, part = sem("wb_in"), sem("freq_ready"), sem("turns_part")
        turns_ready, meta_ready, emb_ready = sem("turns_ready"), sem("meta_ready"), sem("emb_ready")
        sent = [[sem(f"sent{d}{h}") for h in range(2)] for d in range(2)]

        def loop(eng, body):
            body(0)
            with eng.Fori(1, NG // 2) as it:
                body(it)

        def all_sent(eng, d):
            for h in range(2):
                eng.wait_ge(sent[d][h], 16 * CG * (NG // 2))

        with nc.Block() as block:
            @block.sync
            def _(sp):
                sp.dma_start(wb[:, 0, :], w_time.partition_broadcast(EP)).then_inc(wb_in, 16)
                sp.dma_start(wb[:, 1, :], b_time.partition_broadcast(EP)).then_inc(wb_in, 16)

                by_partition = records[0:E, :].rearrange("(p c) r -> p c r", p=EP)

                def body(it):
                    for h in range(2):
                        i = 2 * it + h
                        wait_apart(sp, passed[0], (emb_ready, i + 1))
                        wait_apart(sp, passed[0], (meta_ready, 2 * i + 2))
                        sp.dma_start(by_partition[:, at(i * CG, CG), :], rec[h][:, 0, :, :]
                                     ).then_inc(sent[0][h], 16)
                        sp.sem_inc(sent[0][h], 16 * (CG - 1))
                falls_in = sp.value_load(unsorted[0:1, 0:1], min_val=0, max_val=E)
                with sp.If(falls_in < 1):
                    loop(sp, body)
                all_sent(sp, 0)

            @block.vector
            def _(dve):
                dve.wait_ge(wb_in, 32)
                nc.vector.tensor_scalar(freq[:, 0, :], wb[:, 0, :], float(1 / (2 * np.pi)), None,
                                        ALU.mult).then_inc(freq_ready, 1)
                nc.vector.tensor_scalar(freq[:, 1, :], wb[:, 1, :], float(1 / (2 * np.pi)), 0.25,
                                        ALU.mult, ALU.add).then_inc(freq_ready, 1)
                dve.wait_ge(freq_ready, 2)

                def body(it):
                    for h in range(2):
                        i = 2 * it + h
                        c0 = i * CG
                        shape = [EP, CG, 3, TD]
                        wait(dve, emb_ready, i - 1)
                        nc.vector.tensor_tensor(
                            turns[h][:], log_time[:, at(c0, CG), :].unsqueeze(3).broadcast_to(shape),
                            freq[:, 0:1, :].unsqueeze(1).broadcast_to(shape), ALU.mult).then_inc(part, 1)
                        dve.wait_ge(part, 3 * i + 1)
                        nc.vector.tensor_tensor(
                            turns[h][:], turns[h][:],
                            freq[:, 1:2, :].unsqueeze(1).broadcast_to(shape), ALU.add).then_inc(part, 1)
                        dve.wait_ge(part, 3 * i + 2)
                        nc.vector.tensor_scalar(whole_turns[h][:], turns[h][:], ROUND, -ROUND, ALU.add,
                                                ALU.add).then_inc(part, 1)
                        dve.wait_ge(part, 3 * i + 3)
                        nc.vector.tensor_tensor(turns[h][:], turns[h][:], whole_turns[h][:],
                                                ALU.subtract).then_inc(turns_ready, 1)
                        for d in range(2):
                            wait(dve, sent[d][h], 16 * CG * it)
                        nc.vector.tensor_copy(rec[h][:, :, :, 0:2].bitcast(I32),
                                              meta[:, :, at(c0, CG), :]).then_inc(meta_ready, 1)
                        nc.vector.tensor_copy(idx[h][:], slot[:, :, at(c0, CG)]).then_inc(meta_ready, 1)
                loop(dve, body)

            @block.scalar
            def _(act):
                def body(it):
                    for h in range(2):
                        i = 2 * it + h
                        act.wait_ge(turns_ready, i + 1)
                        for d in range(2):
                            wait(act, sent[d][h], 16 * CG * it)
                        emb = rec[h][:, :, :, 2:REC].rearrange("p d c (t w) -> p d c t w", w=TD)
                        nc.scalar.activation(emb[:, 0, :, :, :], turns[h][:], ACT.Sin, scale=TWO_PI)
                        for place, time in enumerate((0, 2, 1)):
                            ins = nc.scalar.activation(emb[:, 1, :, place, :], turns[h][:, :, time, :],
                                                       ACT.Sin, scale=TWO_PI)
                        ins.then_inc(emb_ready, 1)
                loop(act, body)

            @block.gpsimd
            def _(pool):
                def scatter(directions):
                    def body(it):
                        for h in range(2):
                            i = 2 * it + h
                            wait_apart(pool, passed[1], (emb_ready, i + 1), (meta_ready, 2 * i + 2))
                            for c in range(CG):
                                for d in directions:
                                    nc.gpsimd.indirect_dma_start(
                                        records, bass.IndirectOffsetOnAxis(idx[h][:, d, c:c + 1], 0),
                                        rec[h][:, d, c, :], None).then_inc(sent[d][h], 16)
                    return body

                falls_in = pool.value_load(unsorted[0:1, 0:1], min_val=0, max_val=E)
                with pool.If(falls_in > 0):
                    loop(pool, scatter((0, 1)))
                with pool.Else():
                    loop(pool, scatter((1,)))
                all_sent(pool, 1)
        ctx.close()

    def attention():
        outer = ExitStack()
        ctx = ExitStack()
        acc = outer.enter_context(nc.sbuf_tensor("acc", [BLK, BINS, RHS], F32))

        def sb(name, shape, dt):
            return ctx.enter_context(nc.sbuf_tensor(name, shape, dt))

        def several(depth, name, shape, dt):
            copies = [sb(f"{name}{n}", shape, dt) for n in range(depth)]
            return [copies[j % depth] for j in range(UN)]

        pick = sb("pick", [P, HEADS, BLK], BF16)
        eight = sb("eight", [P, 2 * HEADS], F32)
        pick_f = sb("pick_f", [P, HEADS], F32)
        less_one = sb("less_one", [P, 1], F32)

        LONG, SHORT, TWO = 8, 4, 2
        rec = several(LONG, "arec", [P, 2, REC], F32)
        kv = several(LONG, "akv", [P, 2, 2 * KW], F32)
        hot = several(LONG, "hot", [P, 2, BLK], F32)
        qblk = several(SHORT, "qblk", [BLK, 3, DK], BF16)
        place = several(SHORT, "place", [P, 2], F32)
        mixed = several(SHORT, "mixed", [P, 2, P], BF16)
        hotT = several(SHORT, "hotT", [BLK, 2, P], BF16)
        qs = several(SHORT, "qs", [P, 2, DK], F32)
        score = several(SHORT, "score", [P, 2, HEADS], F32)
        newtop = several(SHORT, "newtop", [BLK, HEADS], F32)
        topparts = several(SHORT, "topparts", [BLK, 2, HEADS], BF16)
        drop = several(SHORT, "drop", [BLK, HEADS], F32)
        keepf = several(SHORT, "keepf", [BLK, HEADS], F32)
        below = several(SHORT, "below", [P, 2, HEADS], F32)
        rhs = several(SHORT, "rhs", [P, 2, RHS], F32)
        mixedT = several(TWO, "mixedT", [P, 2, P], BF16)
        prod = several(TWO, "prod", [P, 2, KW], F32)
        tmax = several(TWO, "tmax", [BLK, HEADS], F32)

        def bank(name, shape):
            return ctx.enter_context(nc.psum_tensor(name, shape, F32))

        hotT_ps = bank("hotT_ps", [P, 4, P])[0:BLK, 0:2, :]
        q_ps = bank("q_ps", [P, 512])[:, 0:2 * DK].rearrange("p (t d) -> p t d", t=2)
        top_ps = bank("top_ps", [P, 512])[:, 0:2 * HEADS].rearrange("p (t h) -> p t h", t=2)
        mixedT_ps = bank("mixedT_ps", [P, 4, P])[:, 0:2, :]
        wide = bank("wide", [P, HEADS, 2, P])[0:BLK]
        sums_ps = [bank(f"sums_ps{b}", [P, 512])[0:BLK, 0:RHS] for b in range(2)]

        rec_in = [sem(f"rec_in{j}") for j in range(UN)]
        q_in = [sem(f"q_in{j}") for j in range(UN)]
        kv_in = [sem(f"kv_in{j}") for j in range(UN)]
        ready, picked = sem("acc_ready"), sem("picked")
        names = ("placed hot_done hot_cast hotT_mm hotT_sb q_mm q_sb eq_added ek_put e0_put prod_done "
                 "score_done hi_done lo_done mixedT_mm mixedT_sb wide_mm tmax_done newtop_done top_hi top_lo "
                 "drop_done top_mm keepf_done dist_done below_done w_done wv_done sums_mm scaled acc_done")
        S = {n: sem(n) for n in names.split()}

        def four(v):
            return v.rearrange("p t (h d) -> p t h d", h=HEADS)

        def loop(eng, order):
            def turn(it, ends):
                for j in range(UN):
                    for stage, lag in order:
                        it2, j2 = it + (j + lag) // UN, (j + lag) % UN
                        if not ends or 0 <= it2 < NS // UN:
                            stage(it2, j2, UN * it2 + j2)

            turn(-1, True)
            turn(0, True)
            with eng.Fori(1, NS // UN - 1) as it:
                turn(it, False)
            turn(NS // UN - 1, True)
            turn(NS // UN, True)

        with nc.Block() as block:
            @block.sync
            def _(sp):
                def load(it, j, k):
                    wait_apart(sp, passed[0], (S["e0_put"], k - LONG + 1), (S["eq_added"], k - LONG + 1))
                    wait_apart(sp, passed[0], (S["q_mm"], k - SHORT + 1))
                    w = sp.value_load(window_of[0:1, at(k)], min_val=0, max_val=2 * E)
                    sp.dma_start(rec[j][:], records[at(w, ST), :].rearrange("(p t) r -> p t r", t=2)
                                 ).then_inc(rec_in[j], 16)
                    b = sp.value_load(block_of[0:1, at(k)], min_val=0, max_val=NBLK - 1)
                    sp.dma_start(qblk[j][:].rearrange("p a d -> p (a d)"), q_table[at(b * BLK, BLK), :]
                                 ).then_inc(q_in[j], 16)
                loop(sp, [(load, 0)])

            @block.gpsimd
            def _(pool):
                nc.gpsimd.memset(acc[:], 0.0).then_inc(ready, 1)
                nc.gpsimd.memset(newtop[UN - 1][:], 0.0).then_inc(ready, 1)

                def add_eq(it, j, k):
                    pool.wait_ge(S["q_sb"], k + 1)
                    nc.gpsimd.tensor_tensor(qs[j][:, :, KQ:DK], qs[j][:, :, KQ:DK],
                                            rec[j][:, :, 2 + 2 * TD:REC], ALU.add).then_inc(S["eq_added"], 1)

                def products(it, j, k):
                    pool.wait_ge(S["eq_added"], k + 1)
                    pool.wait_ge(S["ek_put"], k + 1)
                    wait(pool, S["score_done"], k - TWO + 1)
                    nc.gpsimd.tensor_tensor(four(prod[j][:]), four(kv[j][:, :, 0:KW]),
                                            qs[j][:].unsqueeze(2).broadcast_to([P, 2, HEADS, DK]),
                                            ALU.mult).then_inc(S["prod_done"], 1)

                def gather(it, j, k):
                    wait_apart(pool, passed[2], (rec_in[j], 16 * it + 16), (S["wv_done"], k - LONG + 1),
                               (S["prod_done"], k - LONG + 1))
                    for t in range(2):
                        nc.gpsimd.indirect_dma_start(
                            kv[j][:, t, :], None, kv_table,
                            bass.IndirectOffsetOnAxis(rec[j][:, t, 1:2].bitcast(I32), 0)
                        ).then_inc(kv_in[j], 16)
                loop(pool, [(add_eq, 2), (products, 2), (gather, 5)])

            @block.tensor
            def _(pe):
                def turn_hot(it, j, k):
                    pe.wait_ge(S["hot_done"], k + 1)
                    wait(pe, S["hotT_sb"], k)
                    for t in range(2):
                        mm = nc.tensor.matmul(hotT_ps[:, t, :], mixed[j][:, t, 0:BLK], ident_b[:],
                                              start=True, stop=True)
                    mm.then_inc(S["hotT_mm"], 1)

                def queries(it, j, k):
                    pe.wait_ge(S["hotT_sb"], k + 1)
                    pe.wait_ge(q_in[j], 16 * it + 16)
                    wait(pe, S["q_sb"], k)
                    for t in range(2):
                        for a in range(3):
                            mm = nc.tensor.matmul(q_ps[:, t, :], hotT[j][:, t, :], qblk[j][:, a, :],
                                                  start=(a == 0), stop=(a == 2), skip_group_check=True)
                    mm.then_inc(S["q_mm"], 1)

                def turn_mixed(it, j, k):
                    pe.wait_ge(S["lo_done"], k + 1)
                    wait(pe, S["mixedT_sb"], k)
                    for t in range(2):
                        mm = nc.tensor.matmul(mixedT_ps[:, t, :], mixed[j][:, t, :], ident_b[:],
                                              start=True, stop=True)
                    mm.then_inc(S["mixedT_mm"], 1)

                def spread_scores(it, j, k):
                    pe.wait_ge(S["mixedT_sb"], k + 1)
                    wait(pe, S["tmax_done"], k)
                    for h in range(HEADS):
                        mm = nc.tensor.matmul(wide[:, h, :, :], pick[:, h, :], mixedT[j][:],
                                              start=True, stop=True, skip_group_check=True)
                    mm.then_inc(S["wide_mm"], 1)

                def tops(it, j, k):
                    pe.wait_ge(S["top_lo"], k + 1)
                    wait(pe, S["dist_done"], k)
                    for t in range(2):
                        for a in range(2):
                            mm = nc.tensor.matmul(top_ps[:, t, :], hotT[j][:, t, :], topparts[j][:, a, :],
                                                  start=(a == 0), stop=(a == 1), skip_group_check=True)
                    mm.then_inc(S["top_mm"], 1)

                def sums(it, j, k):
                    pe.wait_ge(S["wv_done"], k + 1)
                    wait(pe, S["acc_done"], k - 1)
                    for t in range(2):
                        mm = nc.tensor.matmul(sums_ps[j % 2], hot[j][:, t, :], rhs[j][:, t, :],
                                              start=(t == 0), stop=(t == 1))
                    mm.then_inc(S["sums_mm"], 1)

                pe.wait_ge(ready, 2)
                pe.wait_ge(picked, 7)
                loop(pe, [(turn_mixed, 1), (sums, -2), (tops, 0), (turn_hot, 3), (spread_scores, 1),
                          (queries, 3)])

            @block.scalar
            def _(act):
                act.wait_ge(picked, 7)

                def locate(it, j, k):
                    act.wait_ge(rec_in[j], 16 * it + 16)
                    wait(act, S["hot_done"], k - SHORT + 1)
                    nc.scalar.activation(place[j][:], rec[j][:, :, 0].bitcast(I32), ACT.Identity,
                                         bias=less_start[:, at(k)]).then_inc(S["placed"], 1)

                def cast_hot(it, j, k):
                    act.wait_ge(S["hot_done"], k + 1)
                    wait(act, S["sums_mm"], k - LONG + 1)
                    nc.scalar.copy(hot[j][:], mixed[j][:, :, 0:BLK]).then_inc(S["hot_cast"], 1)

                def copy_hotT(it, j, k):
                    act.wait_ge(S["hotT_mm"], k + 1)
                    wait(act, S["top_mm"], k - SHORT + 1)
                    nc.scalar.copy(hotT[j][:], hotT_ps).then_inc(S["hotT_sb"], 1)

                def put_ek(it, j, k):
                    act.wait_ge(kv_in[j], 32 * it + 32)
                    act.wait_ge(rec_in[j], 16 * it + 16)
                    nc.scalar.copy(
                        kv[j][:].rearrange("p t (c k) -> p t c k", c=2)[:, :, :, PROJ:KW],
                        rec[j][:, :, 2 + TD:2 + 2 * TD].unsqueeze(2).broadcast_to([P, 2, 2, TD])
                    ).then_inc(S["ek_put"], 1)

                def put_e0(it, j, k):
                    act.wait_ge(rec_in[j], 16 * it + 16)
                    wait(act, S["sums_mm"], k - SHORT + 1)
                    nc.scalar.copy(rhs[j][:, :, HEADS * HW:RHS], rec[j][:, :, 2:2 + TD]
                                   ).then_inc(S["e0_put"], 1)

                def copy_q(it, j, k):
                    act.wait_ge(S["q_mm"], k + 1)
                    wait(act, S["prod_done"], k - SHORT + 1)
                    nc.scalar.copy(qs[j][:], q_ps).then_inc(S["q_sb"], 1)

                def high_part(it, j, k):
                    act.wait_ge(S["score_done"], k + 1)
                    wait(act, S["mixedT_mm"], k - SHORT + 1)
                    nc.scalar.copy(mixed[j][:, :, BLK:BLK + HEADS], score[j][:]).then_inc(S["hi_done"], 1)

                def copy_mixedT(it, j, k):
                    act.wait_ge(S["mixedT_mm"], k + 1)
                    wait(act, S["wide_mm"], k - TWO + 1)
                    nc.scalar.activation(mixedT[j][:], mixedT_ps, ACT.Identity, bias=less_one[:]
                                         ).then_inc(S["mixedT_sb"], 1)

                def top_high(it, j, k):
                    act.wait_ge(S["newtop_done"], k + 1)
                    wait(act, S["top_mm"], k - SHORT + 1)
                    nc.scalar.copy(topparts[j][:, 0, :], newtop[j][:]).then_inc(S["top_hi"], 1)

                def factor(it, j, k):
                    act.wait_ge(S["drop_done"], k + 1)
                    wait(act, S["scaled"], k - SHORT + 1)
                    nc.scalar.activation(keepf[j][:], drop[j][:], ACT.Exp, scale=SCALE
                                         ).then_inc(S["keepf_done"], 1)

                def weights(it, j, k):
                    act.wait_ge(S["below_done"], k + 1)
                    wait(act, S["sums_mm"], k - SHORT + 1)
                    w = rhs[j][:, :, 0:HEADS * HW].rearrange("p t (h d) -> p t h d", h=HEADS)[:, :, :, DK]
                    nc.scalar.activation(w, below[j][:], ACT.Exp, scale=SCALE).then_inc(S["w_done"], 1)

                loop(act, [(copy_mixedT, 1), (put_e0, 0), (top_high, 0), (factor, 0), (put_ek, 3),
                           (cast_hot, 3), (copy_hotT, 3), (high_part, 2), (weights, 0), (copy_q, 3),
                           (locate, 4)])

            @block.vector
            def _(dve):
                nc.vector.tensor_scalar(eight[:], ident[:, BLK:P], 1.0, None, ALU.mult).then_inc(picked, 1)
                nc.vector.tensor_scalar(less_one[:], iota_col[:], float(BLK), -1.0, ALU.is_lt, ALU.mult
                                        ).then_inc(picked, 1)
                dve.wait_ge(picked, 2)
                nc.vector.tensor_tensor(pick_f[:], eight[:, 0:HEADS], eight[:, HEADS:2 * HEADS], ALU.add
                                        ).then_inc(picked, 1)
                dve.wait_ge(picked, 3)
                for h in range(HEADS):
                    nc.vector.scalar_tensor_tensor(pick[:, h, :], ident[:, 0:BLK], BIG,
                                                   pick_f[:, h:h + 1].broadcast_to([P, BLK]),
                                                   ALU.mult, ALU.add).then_inc(picked, 1)
                dve.wait_ge(ready, 2)
                dve.wait_ge(picked, 7)
                reg = {}

                def load_bin(it, j, k):
                    reg["bin"] = dve.value_load(bin_of[0:1, at(k)], min_val=0, max_val=BINS - 1)

                def one_hot(it, j, k):
                    dve.wait_ge(S["placed"], k + 1)
                    wait(dve, S["mixedT_mm"], k - SHORT + 1)
                    wait(dve, S["hot_cast"], k - SHORT + 1)
                    nc.vector.tensor_tensor(mixed[j][:, :, 0:BLK],
                                            iota_row[:, 0:BLK].unsqueeze(1).broadcast_to([P, 2, BLK]),
                                            place[j][:].unsqueeze(2).broadcast_to([P, 2, BLK]),
                                            ALU.is_equal).then_inc(S["hot_done"], 1)

                def scores(it, j, k):
                    dve.wait_ge(S["prod_done"], k + 1)
                    wait(dve, S["dist_done"], k - SHORT + 1)
                    nc.vector.tensor_reduce(score[j][:], four(prod[j][:]), AX.X, ALU.add
                                            ).then_inc(S["score_done"], 1)

                def low_part(it, j, k):
                    dve.wait_ge(S["hi_done"], k + 1)
                    dve.wait_ge(S["score_done"], k + 1)
                    nc.vector.tensor_tensor(mixed[j][:, :, BLK + HEADS:P], score[j][:],
                                            mixed[j][:, :, BLK:BLK + HEADS], ALU.subtract
                                            ).then_inc(S["lo_done"], 1)

                def tile_max(it, j, k):
                    dve.wait_ge(S["wide_mm"], k + 1)
                    wait(dve, S["newtop_done"], k - TWO + 1)
                    nc.vector.tensor_reduce(tmax[j][:], wide.rearrange("p h t e -> p h (t e)"),
                                            AX.X, ALU.max).then_inc(S["tmax_done"], 1)

                def new_top(it, j, k):
                    dve.wait_ge(S["tmax_done"], k + 1)
                    wait(dve, S["newtop_done"], k)
                    wait(dve, S["top_lo"], k - SHORT + 1)
                    nc.vector.scalar_tensor_tensor(newtop[j][:], newtop[j - 1][:],
                                                   carried[0:BLK, at(k)], tmax[j][:], ALU.min, ALU.max
                                                   ).then_inc(S["newtop_done"], 1)

                def top_drop(it, j, k):
                    dve.wait_ge(S["newtop_done"], k + 1)
                    wait(dve, S["keepf_done"], k - SHORT + 1)
                    nc.vector.scalar_tensor_tensor(drop[j][:], newtop[j - 1][:], carried[0:BLK, at(k)],
                                                   newtop[j][:], ALU.min, ALU.subtract
                                                   ).then_inc(S["drop_done"], 1)

                def top_low(it, j, k):
                    dve.wait_ge(S["top_hi"], k + 1)
                    nc.vector.tensor_tensor(topparts[j][:, 1, :], newtop[j][:], topparts[j][:, 0, :],
                                            ALU.subtract).then_inc(S["top_lo"], 1)

                def distance(it, j, k):
                    dve.wait_ge(S["top_mm"], k + 1)
                    wait(dve, S["w_done"], k - SHORT + 1)
                    nc.vector.tensor_tensor(below[j][:], score[j][:], top_ps, ALU.subtract
                                            ).then_inc(S["dist_done"], 1)

                def clamp(it, j, k):
                    dve.wait_ge(S["dist_done"], k + 1)
                    nc.vector.tensor_scalar(below[j][:], below[j][:], 64.0, None, ALU.min
                                            ).then_inc(S["below_done"], 1)

                def weigh(it, j, k):
                    dve.wait_ge(S["w_done"], k + 1)
                    dve.wait_ge(S["ek_put"], k + 1)
                    dve.wait_ge(S["e0_put"], k + 1)
                    r = rhs[j][:, :, 0:HEADS * HW].rearrange("p t (h d) -> p t h d", h=HEADS)
                    nc.vector.tensor_tensor(r[:, :, :, 0:DK], four(kv[j][:, :, KW:2 * KW]),
                                            r[:, :, :, DK:HW].broadcast_to([P, 2, HEADS, DK]),
                                            ALU.mult).then_inc(S["wv_done"], 1)

                def rescale(it, j, k):
                    dve.wait_ge(S["keepf_done"], k + 1)
                    wait(dve, S["acc_done"], k)
                    mine = acc[:, at(reg["bin"]), 0:HEADS * HW].rearrange("p o (h d) -> p (o h) d", h=HEADS)
                    nc.vector.tensor_tensor(mine, mine, keepf[j][:].unsqueeze(2).broadcast_to([BLK, HEADS, HW]),
                                            ALU.mult).then_inc(S["scaled"], 1)

                def add(it, j, k):
                    dve.wait_ge(S["scaled"], k + 1)
                    dve.wait_ge(S["sums_mm"], k + 1)
                    mine = acc[:, at(reg["bin"]), :].rearrange("p o n -> p (o n)")
                    nc.vector.tensor_tensor(mine, mine, sums_ps[j % 2], ALU.add).then_inc(S["acc_done"], 1)

                loop(dve, [(tile_max, 0), (load_bin, -2), (one_hot, 3), (new_top, 0), (rescale, -2),
                           (top_drop, 0), (top_low, 0), (weigh, -1), (scores, 2), (distance, 0), (add, -2),
                           (clamp, 0), (low_part, 2)])
        ctx.close()

        inv = outer.enter_context(nc.sbuf_tensor("inv", [BLK, BINS, HEADS], F32))
        agg = outer.enter_context(nc.sbuf_tensor("agg", [BLK, NBLK, D], F32))
        fin, agg_ready, agg_stored = sem("normalised"), sem("agg_ready"), sem("agg_stored")
        HB = NBLK // 2
        with nc.Block() as block:
            @block.vector
            def _(dve):
                by_head = acc[:, :, 0:HEADS * HW].rearrange("p b (h d) -> p b h d", h=HEADS)
                nc.vector.tensor_scalar(inv[:], by_head[:, :, :, DK], 1e-16, None, ALU.add).then_inc(fin, 1)
                dve.wait_ge(fin, 1)
                nc.vector.reciprocal(inv[:], inv[:]).then_inc(fin, 1)
                dve.wait_ge(fin, 2)
                nc.vector.tensor_tensor(by_head[:, :, :, 0:DK], by_head[:, :, :, 0:DK],
                                        inv[:].unsqueeze(3).broadcast_to([BLK, BINS, HEADS, DK]),
                                        ALU.mult).then_inc(fin, 1)
                dve.wait_ge(fin, 3)
                for b0, b1 in ((0, HB), (HB, NBLK)):
                    nc.vector.tensor_tensor(
                        agg[:, b0:b1, 0:KW].rearrange("p b (h d) -> p b h d", h=HEADS),
                        by_head[:, b0:b1, :, 0:DK], by_head[:, NBLK + b0:NBLK + b1, :, 0:DK],
                        ALU.add).then_inc(agg_ready, 1)
                    nc.vector.tensor_tensor(agg[:, b0:b1, KW:D], acc[:, b0:b1, HEADS * HW:RHS],
                                            acc[:, NBLK + b0:NBLK + b1, HEADS * HW:RHS],
                                            ALU.add).then_inc(agg_ready, 1)

            @block.sync
            def _(sp):
                agg_rows = agg_table.rearrange("(b p) d -> p b d", p=BLK)
                for n, (b0, b1) in enumerate(((0, HB), (HB, NBLK))):
                    sp.wait_ge(agg_ready, 2 * n + 2)
                    sp.dma_start(agg_rows[:, b0:b1, :], agg[:, b0:b1, :]).then_inc(agg_stored, 16)
                sp.wait_ge(agg_stored, 32)
        outer.close()

    def output():
        ctx = ExitStack()

        def two(name, shape, dt):
            return [ctx.enter_context(nc.sbuf_tensor(f"{name}{h}", shape, dt)) for h in range(2)]

        def two_ps(name, shape):
            return [ctx.enter_context(nc.psum_tensor(f"{name}{h}", shape, F32)) for h in range(2)]

        agg = two("oagg", [P, D], F32)
        xg = two("oxg", [P, D], F32)
        aggT = two("aggT", [P, KC, P], F32)
        wa = two("wa", [P, 2 * KC, D], F32)
        rows = two("rows", [1, 3, D], F32)
        y = two("y", [P, D], F32)
        z = two("z", [P, D], F32)
        res = two("res", [P, D], F32)
        stats = two("stats", [P, 6], F32)
        moments = two("moments", [P, 2], F32)
        root = two("root", [P, 1], F32)
        eps = ctx.enter_context(nc.sbuf_tensor("eps", [P, 1], F32))
        aggT_ps = two_ps("aggT_ps", [P, 512])
        y_ps = two_ps("y_ps", [P, 512])
        gb_ps = two_ps("gb_ps", [P, 512])

        wa_in = [sem("wa_in0"), sem("wa_in1")]
        in_ = [sem("nodes_in0"), sem("nodes_in1")]
        stored = [sem("out_stored0"), sem("out_stored1")]
        turned, turned_sb, y_mm = sem("agg_turned"), sem("agg_turned_sb"), sem("y_mm")
        var_ready, root_ready, norm, res_ready = sem("var_ready"), sem("root_ready"), sem("norm"), sem("res_ready")
        eps_set = sem("eps_set")

        def loop(eng, body):
            body(0)
            with eng.Fori(1, NT // 2) as it:
                body(it)

        with nc.Block() as block:
            @block.sync
            def _(sp):
                def body(it):
                    for h in range(2):
                        i = 2 * it + h
                        wait(sp, y_mm, i - 1)
                        t = sp.value_load(type_of[0:1, at(i)], min_val=0, max_val=T - 1)
                        sp.dma_start(wa[h][:], Wa[at(t)].rearrange("o (c k) n -> k (o c) n", k=P)
                                     ).then_inc(wa_in[h], 16)
                        for c, b in enumerate((ba, gamma, beta)):
                            sp.dma_start(rows[h][:, c, :], b[at(t), :]).then_inc(wa_in[h], 16)
                loop(sp, body)

            @block.gpsimd
            def _(pool):
                nc.gpsimd.memset(eps[:], LN_EPS).then_inc(eps_set, 1)

                def gather(i):
                    wait(pool, res_ready, i - 1)
                    for tile_, table in ((agg, agg_table), (xg, x)):
                        nc.gpsimd.indirect_dma_start(
                            tile_[i % 2][:], None, table,
                            bass.IndirectOffsetOnAxis(node_ids[:, i, 1:2], 0)).then_inc(in_[i % 2], 16)

                gather(0)
                for i in range(NT):
                    if i + 1 < NT:
                        gather(i + 1)
                    pool.wait_ge(res_ready, i + 1)
                    nc.gpsimd.indirect_dma_start(
                        out, bass.IndirectOffsetOnAxis(node_ids[:, i, 0:1], 0), res[i % 2][:], None,
                        bounds_check=N - 1, oob_is_err=False).then_inc(stored[i % 2], 16)
                for h in range(2):
                    pool.wait_ge(stored[h], 16 * (NT // 2))

            @block.tensor
            def _(pe):
                def body(it):
                    for h in range(2):
                        i = 2 * it + h
                        pe.wait_ge(in_[h], 32 * it + 32)
                        wait(pe, turned_sb, i - 1)
                        for c in range(KC):
                            mm = nc.tensor.transpose(aggT_ps[h][:, c * P:(c + 1) * P],
                                                     agg[h][:, c * P:(c + 1) * P], ident[:])
                        mm.then_inc(turned, 1)
                        pe.wait_ge(wa_in[h], 64 * it + 64)
                        pe.wait_ge(turned_sb, i + 1)
                        wait(pe, res_ready, i - 1)
                        nc.tensor.matmul(gb_ps[h][:], ones[0:1, :],
                                         rows[h][:, 1:3, :].rearrange("p c n -> p (c n)"),
                                         start=True, stop=True)
                        nc.tensor.matmul(y_ps[h][:, 0:D], ones[0:1, :], rows[h][:, 0, :],
                                         start=True, stop=False)
                        for c in range(2 * KC):
                            mm = nc.tensor.matmul(y_ps[h][:, 0:D], aggT[h][:, c % KC, :], wa[h][:, c, :],
                                                  start=False, stop=(c == 2 * KC - 1))
                        mm.then_inc(y_mm, 1)
                loop(pe, body)

            @block.scalar
            def _(act):
                act.wait_ge(eps_set, 1)

                def body(it):
                    for h in range(2):
                        i = 2 * it + h
                        act.wait_ge(turned, i + 1)
                        wait(act, y_mm, i - 1)
                        nc.scalar.copy(aggT[h][:],
                                       aggT_ps[h][:, 0:KC * P].rearrange("p (c k) -> p c k", c=KC)
                                       ).then_inc(turned_sb, 1)
                        for n in range(2):
                            act.wait_ge(var_ready, 2 * i + n + 1)
                            nc.scalar.activation(root[h][:], moments[h][:, 1:2], ACT.Sqrt,
                                                 bias=eps[:]).then_inc(root_ready, 1)
                loop(act, body)

            @block.vector
            def _(dve):
                def body(it):
                    for h in range(2):
                        i = 2 * it + h
                        done = [0]

                        def step(ins):
                            done[0] += 1
                            ins.then_inc(norm, 1)
                            wait_apart(dve, passed[3], (norm, 9 * i + done[0]))

                        def normalised(a, into, n):
                            step(nc.vector.bn_stats(stats[h][:], a))
                            nc.vector.bn_aggr(moments[h][:], stats[h][:]).then_inc(var_ready, 1)
                            dve.wait_ge(root_ready, 2 * i + n + 1)
                            step(nc.vector.reciprocal(root[h][:], root[h][:]))
                            step(nc.vector.tensor_scalar(into, a, moments[h][:, 0:1], root[h][:, 0:1],
                                                         ALU.subtract, ALU.mult))

                        dve.wait_ge(y_mm, i + 1)
                        dve.wait_ge(in_[h], 32 * it + 32)
                        step(nc.vector.tensor_tensor(y[h][:], y_ps[h][:, 0:D], xg[h][:], ALU.add))
                        normalised(y[h][:], z[h][:], 0)
                        step(nc.vector.tensor_tensor(z[h][:], z[h][:], gb_ps[h][:, 0:D], ALU.mult))
                        step(nc.vector.tensor_tensor(z[h][:], z[h][:], gb_ps[h][:, D:2 * D], ALU.add))
                        step(nc.vector.tensor_tensor(y[h][:], z[h][:], xg[h][:], ALU.add))
                        step(nc.vector.bn_stats(stats[h][:], y[h][:]))
                        nc.vector.bn_aggr(moments[h][:], stats[h][:]).then_inc(var_ready, 1)
                        dve.wait_ge(root_ready, 2 * i + 2)
                        step(nc.vector.reciprocal(root[h][:], root[h][:]))
                        wait(dve, stored[h], 16 * it)
                        nc.vector.tensor_scalar(res[h][:], y[h][:], moments[h][:, 0:1], root[h][:, 0:1],
                                                ALU.subtract, ALU.mult).then_inc(res_ready, 1)
                        STEPS[0] = done[0]
                STEPS = [0]
                loop(dve, body)
        ctx.close()

    sort()
    nodes()
    edges()
    early.close()
    attention()
    output()
    whole.close()


_INS = ['x', 'src', 'dst', 'edge_attr_5', 'node_type_19', 'L0_gnn_Wk', 'L0_gnn_bk', 'L0_gnn_Wq', 'L0_gnn_bq',
        'L0_gnn_Wv', 'L0_gnn_bv', 'L0_gnn_Wa', 'L0_gnn_ba', 'L0_gnn_gamma', 'L0_gnn_beta', 'L0_gnn_w_time',
        'L0_gnn_b_time']


def kernel(**inputs):
    import numpy as _np
    import concourse.bacc as _bacc
    from concourse import mybir as _mybir
    from concourse.bass_utils import run_bass_kernel_spmd as _run

    nc = _bacc.Bacc("TRN2", target_bir_lowering=False, num_devices=1)
    arrays, args = {}, []
    for name in _INS:
        a = _np.ascontiguousarray(inputs[name])
        arrays[f"in_{name}_dram"] = a
        args.append(nc.dram_tensor(f"in_{name}_dram", a.shape, _mybir.dt.from_np(a.dtype), kind="ExternalInput").ap())
    shape = inputs['x'].shape
    args.append(nc.dram_tensor("out_0_dram", list(shape), _mybir.dt.float32, kind="ExternalOutput").ap())
    gnn_kernel(nc, *args)
    r = _run(nc, [arrays], core_ids=[0])
    return r.results[0]["out_0_dram"]
```

```python
from contextlib import ExitStack

import numpy as np

import concourse.bass as bass
from concourse import mybir

ALU = mybir.AluOpType
ACT = mybir.ActivationFunctionType
AX = mybir.AxisListType
F32 = mybir.dt.float32
BF16 = mybir.dt.bfloat16
I32 = mybir.dt.int32
U32 = mybir.dt.uint32

P = 128
HEADS = 4
TD = 32
BIG = float(2.0**100)
ROUND = 1.5 * 2.0**23
TWO_PI = 6.2831845
LN_EPS = 1e-5
BLK = P - 2 * HEADS
UN = 8
CG = 8


def wait(eng, sem, value):
    if not (isinstance(value, int) and value <= 0):
        eng.wait_ge(sem, value)


def wait_apart(eng, mark, *waits):
    for s, v in waits:
        wait(eng, s, v)
    eng.sem_inc(mark, 1)


def at(base, n=1):
    return bass.ds(base, n)


def gnn_kernel(nc, x, src, dst, edge_attr, node_type, Wk, bk, Wq, bq, Wv, bv, Wa, ba, gamma, beta,
               w_time, b_time, out):
    N, D = x.shape
    E = src.shape[0]
    T, _, PROJ = Wk.shape
    DK = (PROJ + TD) // HEADS
    KW = HEADS * DK
    KQ = PROJ - 3 * DK
    SCALE = 1.0 / float(np.sqrt(DK))
    KC = D // P

    EP = max(p for p in range(1, P + 1) if E % p == 0)
    EC = E // EP
    NP_ = max(p for p in range(1, P + 1) if N % p == 0)
    NCOL = N // NP_
    NBLK = -(-N // BLK)
    BINS = 2 * NBLK
    ST = 2 * P
    NS = (2 * E + BINS * (ST - 1)) // ST
    NS = -(-NS // UN) * UN
    NT = (N + T * (P - 1)) // P
    NT = -(-NT // 4) * 4
    NPAD = NBLK * BLK
    assert NPAD - N <= P
    REC = 2 + 3 * TD
    HW = DK + 1
    RHS = HEADS * HW + TD
    NG = EC // CG
    assert EC % (2 * CG) == 0 and D == 2 * P and NS % UN == 0

    records = nc.dram_tensor("records", [2 * E + ST, REC], F32).ap()
    node_slots = nc.dram_tensor("node_slots", [NT * P, 2], I32).ap()
    kv_table = nc.dram_tensor("kv_table", [N, 2 * KW], F32).ap()
    q_table = nc.dram_tensor("q_table", [NPAD, 3 * DK], BF16).ap()
    agg_table = nc.dram_tensor("agg_table", [NPAD, D], F32).ap()

    whole = ExitStack()
    early = ExitStack()

    def sem(name):
        return whole.enter_context(nc.semaphore(name))

    def keep(name, shape, dt):
        return whole.enter_context(nc.sbuf_tensor(name, shape, dt))

    def edge_keep(name, shape, dt):
        return early.enter_context(nc.sbuf_tensor(name, shape, dt))

    passed = [sem(f"passed{i}") for i in range(4)]

    iota_row = keep("iota_row", [P, P], F32)
    iota_col = keep("iota_col", [P, 1], F32)
    ident = keep("ident", [P, P], F32)
    ident_b = keep("ident_b", [P, P], BF16)
    ones = keep("ones", [P, P], F32)
    bin_of = keep("bin_of", [1, NS], I32)
    window_of = keep("window_of", [1, NS], I32)
    less_start = keep("less_start", [P, NS], F32)
    carried = keep("carried", [P, NS], F32)
    block_of = keep("block_of", [1, NS], I32)
    type_of = keep("type_of", [1, NT], I32)
    node_ids = keep("node_ids", [P, NT, 2], I32)

    unsorted = keep("unsorted", [1, 1], I32)

    meta = edge_keep("meta", [EP, 2, EC, 2], I32)
    slot = edge_keep("slot", [EP, 2, EC], I32)
    log_time = edge_keep("log_time", [EP, EC, 3], F32)

    def prepare():
        ctx = ExitStack()

        def sb(name, shape, dt):
            return ctx.enter_context(nc.sbuf_tensor(name, shape, dt))

        def ps(name, shape):
            return ctx.enter_context(nc.psum_tensor(name, shape, F32))

        ends = sb("ends", [EP, 2, EC], I32)
        key = sb("key", [EP, 2, EC], F32)
        flag = sb("flag", [EP, EC], F32)
        next_dst = sb("next_dst", [EP, 2], I32)
        falls = sb("falls", [EP, 1], F32)
        cum = sb("cum", [EP, EC], F32)
        pos = sb("pos", [EP, 2, EC], F32)
        times = sb("times", [EP, EC, 5], F32)
        ntype = sb("ntype", [NP_, NCOL], I32)
        nkey = sb("nkey", [NP_, NCOL], F32)
        nflag = sb("nflag", [NP_, NCOL], F32)
        ncum = sb("ncum", [NP_, NCOL], F32)
        npos = sb("npos", [NP_, NCOL], F32)
        nslot = sb("nslot", [NP_, NCOL], I32)
        nrec = sb("nrec", [NP_, NCOL, 2], I32)
        nfill = sb("nfill", [P, NT, 2], I32)
        fill = sb("fill", [P, ST // P, REC], F32)
        before = sb("before", [P, P], F32)
        iota_u = sb("iota_u", [P, NS], F32)
        counts = [sb("ecount", [P, BINS], F32), sb("ncount", [P, T], F32)]
        tiles_i = [sb("etiles_i", [P, BINS], I32), sb("ntiles_i", [P, T], I32)]
        tiles = [sb("etiles", [P, BINS], F32), sb("ntiles", [P, T], F32)]
        upto = [sb("eupto", [P, BINS], F32), sb("nupto", [P, T], F32)]
        first = [sb("efirst", [P, BINS], F32), sb("nfirst", [P, T], F32)]
        base = [sb("ebase", [P, BINS], F32), sb("nbase", [P, T], F32)]
        first_col = [sb("efirst_col", [P, 1], F32), sb("nfirst_col", [P, 1], F32)]
        begun = [sb("ebegun", [P, NS], F32), sb("nbegun", [P, NT], F32)]
        row = sb("row", [1, NS], F32)
        row2 = sb("row2", [1, NS], F32)
        edges_upto = sb("edges_upto", [P, BINS], F32)
        edges_before = sb("edges_before", [P, BINS], F32)
        shift = sb("shift", [1, 1 + BINS], F32)
        rise = sb("rise", [1, BINS], F32)
        rise_col = sb("rise_col", [P, 1], F32)
        total = sb("total", [P, BINS], F32)

        def two(name, shape, dt):
            return [sb(f"{name}{h}", shape, dt) for h in range(2)]

        xg = [sb(f"xg{g}", [P, D], F32) for g in range(4)]
        xT = two("xT", [P, KC, P], F32)
        w = two("w", [P, KC, 3 * PROJ], F32)
        bias = two("bias", [1, 3 * PROJ], F32)
        kv = two("kv", [P, 2, KW], F32)
        q = two("q", [P, DK], F32)
        qh = two("qh", [P, PROJ], F32)
        q3 = two("q3", [P, 3, DK], BF16)
        zeros = sb("zeros", [NPAD - N, 3 * DK], BF16)
        xT_ps = [ps(f"xT_ps{h}", [P, 512]) for h in range(2)]
        kv_ps = [ps(f"kv_ps{h}", [P, 512]) for h in range(2)]
        q_ps = [ps(f"q_ps{h}", [P, 512]) for h in range(2)]

        bank = [ps("esort_ps", [P, 512]), ps("nsort_ps", [P, 512])]
        off_ps = [bank[0][:, 0:BINS], bank[1][:, 0:T]]
        tot_ps = [bank[0][:, P:P + BINS], bank[1][:, P:P + T]]
        falls_ps = bank[0][0:1, 2 * P:2 * P + 1]
        rise_ps = bank[0][0:BINS, 2 * P + 2:2 * P + 3]
        first_ps = [bank[0][0:BINS, 2 * P + 1:2 * P + 2], bank[1][0:T, 2 * P + 1:2 * P + 2]]
        type_ps = bank[1][0:1, 3 * P:3 * P + NT]
        half = NS // 2
        assert half <= 512 and BINS <= P and NT <= P
        map_ps = [bank[0][:, 0:half], bank[1][:, 0:half]]

        ends_in, times_in, ntype_in = sem("ends_in"), sem("times_in"), sem("ntype_in")
        pool_done, fill_ready, filled = sem("pool_done"), sem("fill_ready"), sem("filled")
        nfilled, nslot_ready, nscattered = sem("nfilled"), sem("nslot_ready"), sem("nscattered")
        ids_in, dve_done, logs = sem("ids_in"), sem("dve_done"), sem("logs")
        counted, summed, first_ready, cols_done = sem("counted"), sem("summed"), sem("first_ready"), sem("cols_done")
        begun_ready, maps_done, map_read = sem("begun_ready"), sem("maps_done"), sem("map_read")
        slots_done, type_ready, tail_stored = sem("slots_done"), sem("type_ready"), sem("tail_stored")
        w_in = [sem("w_in0"), sem("w_in1")]
        x_in = [sem(f"x_in{g}") for g in range(4)]
        stored = [sem("kv_stored0"), sem("kv_stored1")]
        gaps, turned, turned_sb = sem("gaps"), sem("turned"), sem("turned_sb")
        projected, kv_ready, q_sum, q_ready = sem("projected"), sem("kv_ready"), sem("q_sum"), sem("q_ready")
        q_copied = sem("q_copied")
        MID = NT // 8 + 1

        with nc.Block() as block:
            @block.sync
            def _(sp):
                sp.dma_start(ntype[:], node_type.rearrange("(p c) -> p c", p=NP_)).then_inc(ntype_in, 16)
                sp.dma_start(ends[:, 0, :], dst.rearrange("(p c) -> p c", p=EP)).then_inc(ends_in, 16)
                sp.dma_start(ends[:, 1, :], src.rearrange("(p c) -> p c", p=EP)).then_inc(ends_in, 16)
                sp.wait_ge(pool_done, 1)
                sp.dma_start(next_dst[0:EP - 1, :], dst.rearrange("(p c) -> p c", p=EP)[1:EP, 0:2]
                             ).then_inc(ends_in, 16)
                sp.dma_start(times[:], edge_attr.rearrange("(p c) k -> p c k", p=EP)).then_inc(times_in, 16)
                sp.wait_ge(fill_ready, 1)
                sp.dma_start(records[2 * E:2 * E + ST, :].rearrange("(p n) r -> p n r", p=P), fill[:]
                             ).then_inc(filled, 16)
                slots_by_p = node_slots.rearrange("(i p) c -> p i c", p=P)
                sp.dma_start(slots_by_p, nfill[:]).then_inc(nfilled, 16)
                sp.wait_ge(gaps, 3)
                sp.dma_start(q_table[N:NPAD, :], zeros[:]).then_inc(tail_stored, 16)
                sp.wait_ge(nscattered, 16 * NCOL)
                sp.dma_start(node_ids[:], slots_by_p).then_inc(ids_in, 16)
                sp.wait_ge(type_ready, 1)

                def body(it):
                    for h in range(2):
                        i = 2 * it + h
                        wait(sp, projected, i - 1)
                        t = sp.value_load(type_of[0:1, at(i)], min_val=0, max_val=T - 1)
                        for c, (W, b) in enumerate(((Wk, bk), (Wv, bv), (Wq, bq))):
                            sp.dma_start(w[h][:, :, c * PROJ:(c + 1) * PROJ],
                                         W[at(t)].rearrange("o (c k) n -> k (o c) n", k=P)
                                         ).then_inc(w_in[h], 16)
                            sp.dma_start(bias[h][:, c * PROJ:(c + 1) * PROJ],
                                         b[at(t), :]).then_inc(w_in[h], 16)
                body(0)
                with sp.Fori(1, NT // 2) as it:
                    body(it)
                sp.wait_ge(tail_stored, 16)
                sp.wait_ge(filled, 16)

            @block.gpsimd
            def _(pool):
                nc.gpsimd.memset(next_dst[:], N).then_inc(pool_done, 1)
                nc.gpsimd.iota(iota_row[:], [[1, P]], base=0, channel_multiplier=0,
                               allow_small_or_imprecise_dtypes=True).then_inc(pool_done, 1)
                nc.gpsimd.iota(iota_col[:], [[1, 1]], base=0, channel_multiplier=1,
                               allow_small_or_imprecise_dtypes=True).then_inc(pool_done, 1)
                nc.gpsimd.iota(iota_u[:], [[1, NS]], base=0, channel_multiplier=0,
                               allow_small_or_imprecise_dtypes=True).then_inc(pool_done, 1)
                nc.gpsimd.memset(ones[:], 1.0).then_inc(pool_done, 1)
                for c in range(2):
                    nc.gpsimd.iota(nrec[:, :, c], [[1, NCOL]], base=0,
                                   channel_multiplier=NCOL).then_inc(pool_done, 1)
                nc.gpsimd.iota(nfill[:, :, 0], [[0, NT]], base=N, channel_multiplier=1).then_inc(pool_done, 1)
                nc.gpsimd.memset(nfill[:, :, 1], 0).then_inc(pool_done, 1)
                nc.gpsimd.memset(fill[:], 0.0).then_inc(pool_done, 1)
                pool.wait_ge(pool_done, 10)
                nc.gpsimd.memset(fill[:, :, 0:1].bitcast(I32), BINS * BLK).then_inc(fill_ready, 1)
                for h in range(2):
                    nc.gpsimd.memset(kv[h][:], 0.0).then_inc(gaps, 1)
                nc.gpsimd.memset(zeros[:], 0.0).then_inc(gaps, 1)
                pool.wait_ge(nslot_ready, 1)
                pool.wait_ge(nfilled, 16)
                for c in range(NCOL):
                    nc.gpsimd.indirect_dma_start(
                        node_slots, bass.IndirectOffsetOnAxis(nslot[:, c:c + 1], 0), nrec[:, c, :],
                        None).then_inc(nscattered, 16)

                pool.wait_ge(ids_in, 16)

                def gather(i):
                    wait(pool, turned, i - 3)
                    nc.gpsimd.indirect_dma_start(
                        xg[i % 4][:], None, x, bass.IndirectOffsetOnAxis(node_ids[:, i, 1:2], 0)
                    ).then_inc(x_in[i % 4], 16)

                def sum_queries(i):
                    h, c = i % 2, [0]
                    full, part = q[h], q3[h]

                    def step(into, one, other, op):
                        c[0] += 1
                        nc.gpsimd.tensor_tensor(into, one, other, op).then_inc(q_sum, 1)
                        pool.wait_ge(q_sum, 6 * i + c[0])

                    pool.wait_ge(projected, i + 1)
                    pool.wait_ge(q_copied, i + 1)
                    wait(pool, stored[h], 32 * (i // 2))
                    step(full[:], qh[h][:, 0:DK], qh[h][:, DK:2 * DK], ALU.add)
                    step(full[:], full[:], qh[h][:, 2 * DK:3 * DK], ALU.add)
                    step(full[:, 0:KQ], full[:, 0:KQ], qh[h][:, 3 * DK:PROJ], ALU.add)
                    step(part[:, 0, :], full[:], ones[:, 0:DK], ALU.mult)
                    step(full[:], full[:], part[:, 0, :], ALU.subtract)
                    step(part[:, 1, :], full[:], ones[:, 0:DK], ALU.mult)
                    nc.gpsimd.tensor_tensor(part[:, 2, :], full[:], part[:, 1, :], ALU.subtract
                                            ).then_inc(q_ready, 1)

                for i in range(3):
                    gather(i)
                for i in range(NT):
                    if i + 3 < NT:
                        gather(i + 3)
                    sum_queries(i)
                    pool.wait_ge(kv_ready, i + 1)
                    nc.gpsimd.indirect_dma_start(
                        kv_table, bass.IndirectOffsetOnAxis(node_ids[:, i, 0:1], 0),
                        kv[i % 2][:].rearrange("p c k -> p (c k)"), None,
                        bounds_check=N - 1, oob_is_err=False).then_inc(stored[i % 2], 16)
                    pool.wait_ge(q_ready, i + 1)
                    nc.gpsimd.indirect_dma_start(
                        q_table, bass.IndirectOffsetOnAxis(node_ids[:, i, 0:1], 0),
                        q3[i % 2][:].rearrange("p a d -> p (a d)"), None,
                        bounds_check=N - 1, oob_is_err=False).then_inc(stored[i % 2], 16)
                for h in range(2):
                    pool.wait_ge(stored[h], 32 * (NT // 2))

            @block.tensor
            def _(pe):
                def sums_of(k, rows, bins):
                    nc.tensor.matmul(off_ps[k][0:rows, :], before[0:rows, 0:rows],
                                     counts[k][0:rows, :], start=True, stop=True).then_inc(summed, 1)
                    nc.tensor.matmul(tot_ps[k], ones[0:rows, :], counts[k][0:rows, :],
                                     start=True, stop=True).then_inc(summed, 1)

                pe.wait_ge(counted, 1)
                sums_of(1, NP_, T)
                pe.wait_ge(first_ready, 1)
                nc.tensor.matmul(first_ps[1], first[1][0:1, :], ones[0:1, 0:1],
                                 start=True, stop=True).then_inc(cols_done, 1)
                pe.wait_ge(begun_ready, 1)
                nc.tensor.matmul(type_ps, ones[0:T, 0:1], begun[1][0:T, :],
                                 start=True, stop=True).then_inc(maps_done, 1)

                def body(it):
                    for g in range(4):
                        i = 4 * it + g
                        h = g % 2
                        pe.wait_ge(x_in[g], 16 * it + 16)
                        wait(pe, turned_sb, i - 1)
                        for c in range(KC):
                            mm = nc.tensor.transpose(xT_ps[h][:, c * P:(c + 1) * P],
                                                     xg[g][:, c * P:(c + 1) * P], ident[:])
                        mm.then_inc(turned, 1)
                        pe.wait_ge(w_in[h], 96 * (2 * it + g // 2) + 96)
                        pe.wait_ge(turned_sb, i + 1)
                        wait(pe, kv_ready, i - 1)
                        wait(pe, q_copied, i - 1)
                        for out_ps, a, b in ((kv_ps[h], 0, 2 * PROJ), (q_ps[h], 2 * PROJ, 3 * PROJ)):
                            nc.tensor.matmul(out_ps[:, 0:b - a], ones[0:1, :], bias[h][:, a:b],
                                             start=True, stop=False)
                            for c in range(KC):
                                mm = nc.tensor.matmul(out_ps[:, 0:b - a], xT[h][:, c, :], w[h][:, c, a:b],
                                                      start=False, stop=(c == KC - 1))
                        mm.then_inc(projected, 1)
                body(0)
                with pe.Fori(1, MID) as it:
                    body(it)

                pe.wait_ge(counted, 2)
                sums_of(0, EP, BINS)
                nc.tensor.matmul(falls_ps, falls[:], ones[0:EP, 0:1],
                                 start=True, stop=True).then_inc(summed, 1)
                pe.wait_ge(first_ready, 2)
                nc.tensor.matmul(first_ps[0], first[0][0:1, :], ones[0:1, 0:1],
                                 start=True, stop=True).then_inc(cols_done, 1)
                nc.tensor.matmul(rise_ps, rise[:], ones[0:1, 0:1],
                                 start=True, stop=True).then_inc(cols_done, 1)
                pe.wait_ge(begun_ready, 2)
                for n2 in range(2):
                    mm = nc.tensor.matmul(map_ps[n2], ones[0:BINS, :],
                                          begun[0][0:BINS, n2 * half:(n2 + 1) * half], start=True, stop=True)
                mm.then_inc(maps_done, 1)
                pe.wait_ge(map_read, 1)
                for n2 in range(2):
                    mm = nc.tensor.matmul(map_ps[n2][0:1, :], rise_col[0:BINS, :],
                                          begun[0][0:BINS, n2 * half:(n2 + 1) * half], start=True, stop=True)
                mm.then_inc(maps_done, 1)

                with pe.Fori(MID, NT // 4) as it:
                    body(it)

            @block.scalar
            def _(act):
                act.wait_ge(times_in, 16)
                nc.scalar.activation(log_time[:], times[:, :, 0:3], ACT.Ln, bias=1.0).then_inc(logs, 1)
                act.wait_ge(logs, 1)
                act.wait_ge(gaps, 3)

                def body(it):
                    for h in range(2):
                        i = 2 * it + h
                        act.wait_ge(turned, i + 1)
                        wait(act, projected, i - 1)
                        nc.scalar.copy(xT[h][:], xT_ps[h][:, 0:KC * P].rearrange("p (c k) -> p c k", c=KC)
                                       ).then_inc(turned_sb, 1)
                        act.wait_ge(projected, i + 1)
                        wait(act, q_ready, i - 1)
                        nc.scalar.copy(qh[h][:], q_ps[h][:, 0:PROJ]).then_inc(q_copied, 1)
                        wait(act, stored[h], 32 * it)
                        nc.scalar.copy(kv[h][:, :, 0:PROJ],
                                       kv_ps[h][:, 0:2 * PROJ].rearrange("p (c k) -> p c k", c=2)
                                       ).then_inc(kv_ready, 1)
                body(0)
                with act.Fori(1, NT // 2) as it:
                    body(it)

            @block.vector
            def _(dve):
                n = [0]

                def step(ins, sem_=dve_done):
                    n[0] += 1
                    ins.then_inc(sem_, 1)
                    dve.wait_ge(sem_, n[0])

                def count(keys, k, b0, bins, fl, rows):
                    with dve.Fori(0, bins) as b:
                        nc.vector.tensor_scalar(fl[:], keys, iota_row[0:rows, at(b)], None,
                                                ALU.is_equal).then_inc(dve_done, 1)
                        dve.wait_ge(dve_done, 2 * b + (n[0] + 1))
                        nc.vector.tensor_reduce(counts[k][0:rows, at(b + b0)], fl[:], AX.X,
                                                ALU.add).then_inc(dve_done, 1)
                        dve.wait_ge(dve_done, 2 * b + (n[0] + 2))
                    n[0] += 2 * bins

                def tiles_from_totals(k, bins, log2):
                    step(nc.vector.tensor_scalar(tiles_i[k][:], tot_ps[k], float(2**log2 - 1), None,
                                                 ALU.add))
                    step(nc.vector.tensor_scalar(tiles_i[k][:], tiles_i[k][:], log2, None,
                                                 ALU.arith_shift_right))
                    step(nc.vector.tensor_copy(tiles[k][:], tiles_i[k][:]))
                    step(nc.vector.tensor_tensor_scan(upto[k][:], tiles[k][:], tiles[k][:], 0.0,
                                                      ALU.add, ALU.max))
                    step(nc.vector.tensor_tensor(first[k][:], upto[k][:], tiles[k][:], ALU.subtract))

                def rank(keys, k, b0, bins, fl, cu, po, rows, into, sem_):
                    step(nc.vector.memset(po, 0.0))
                    with dve.Fori(0, bins) as b:
                        nc.vector.tensor_scalar(fl[:], keys, iota_row[0:rows, at(b)], None,
                                                ALU.is_equal).then_inc(dve_done, 1)
                        dve.wait_ge(dve_done, 3 * b + (n[0] + 1))
                        nc.vector.tensor_tensor_scan(cu[:], fl[:], fl[:], base[k][0:rows, at(b + b0)],
                                                     ALU.add, ALU.max).then_inc(dve_done, 1)
                        wait_apart(dve, passed[0], (dve_done, 3 * b + (n[0] + 2)))
                        nc.vector.copy_predicated(po, fl[:].bitcast(U32), cu[:]).then_inc(dve_done, 1)
                        dve.wait_ge(dve_done, 3 * b + (n[0] + 3))
                    n[0] += 3 * bins
                    nc.vector.tensor_scalar(into, po, -1.0, None, ALU.add).then_inc(sem_, 1)

                dve.wait_ge(pool_done, 10)
                step(nc.vector.tensor_scalar(before[:], iota_row[:], iota_col[:], None, ALU.is_gt))
                step(nc.vector.tensor_scalar(ident[:], iota_row[:], iota_col[:], None, ALU.is_equal))
                step(nc.vector.tensor_copy(ident_b[:], ident[:]))

                dve.wait_ge(ntype_in, 16)
                step(nc.vector.tensor_copy(nkey[:], ntype[:]))
                count(nkey[:], 1, 0, T, nflag, NP_)
                dve.sem_inc(counted, 1)
                dve.wait_ge(summed, 2)
                tiles_from_totals(1, T, 7)
                step(nc.vector.scalar_tensor_tensor(base[1][0:NP_, :], first[1][0:NP_, :], float(P),
                                                    off_ps[1][0:NP_, :], ALU.mult, ALU.add))
                dve.sem_inc(first_ready, 1)
                dve.wait_ge(cols_done, 1)
                step(nc.vector.tensor_copy(first_col[1][0:T, :], first_ps[1]))
                step(nc.vector.tensor_scalar(begun[1][0:T, :], iota_u[0:T, 0:NT], first_col[1][0:T, :],
                                             None, ALU.is_ge))
                dve.sem_inc(begun_ready, 1)
                dve.wait_ge(maps_done, 1)
                nc.vector.tensor_scalar(type_of[:], type_ps, -1.0, None, ALU.add).then_inc(type_ready, 1)
                rank(nkey[:], 1, 0, T, nflag, ncum, npos[:], NP_, nslot[:], nslot_ready)

                dve.wait_ge(ends_in, 48)
                for d in range(2):
                    step(nc.vector.tensor_scalar(key[:, d, :], ends[:, d, :], 1.0 / BLK,
                                                 0.5 / BLK - 0.5, ALU.mult, ALU.add))
                    step(nc.vector.tensor_scalar(key[:, d, :], key[:, d, :], ROUND, -ROUND, ALU.add,
                                                 ALU.add))
                    step(nc.vector.tensor_scalar(meta[:, d, :, 0], ends[:, d, :], float(d * NBLK * BLK),
                                                 None, ALU.add))
                    step(nc.vector.tensor_copy(meta[:, d, :, 1], ends[:, 1 - d, :]))

                step(nc.vector.tensor_tensor(flag[:, 0:EC - 1], ends[:, 0, 0:EC - 1], ends[:, 0, 1:EC],
                                             ALU.is_gt))
                step(nc.vector.tensor_tensor(flag[:, EC - 1:EC], ends[:, 0, EC - 1:EC], next_dst[:, 0:1],
                                             ALU.is_gt))
                step(nc.vector.tensor_reduce(falls[:], flag[:], AX.X, ALU.add))

                for d in range(2):
                    count(key[:, d, :], 0, d * NBLK, NBLK, flag, EP)
                dve.sem_inc(counted, 1)
                dve.wait_ge(summed, 5)
                step(nc.vector.tensor_copy(unsorted[:], falls_ps))
                step(nc.vector.tensor_copy(total[:], tot_ps[0]))
                step(nc.vector.tensor_tensor_scan(edges_upto[:], total[:], total[:], 0.0, ALU.add,
                                                  ALU.max))
                step(nc.vector.tensor_tensor(edges_before[:], edges_upto[:], total[:], ALU.subtract))
                tiles_from_totals(0, BINS, 8)
                step(nc.vector.tensor_tensor(base[0][0:EP, :], edges_before[0:EP, :],
                                             off_ps[0][0:EP, :], ALU.add))
                step(nc.vector.memset(shift[:], 0.0))
                step(nc.vector.scalar_tensor_tensor(shift[:, 1:1 + BINS], first[0][0:1, :], -float(ST),
                                                    edges_before[0:1, :], ALU.mult, ALU.add))
                step(nc.vector.tensor_tensor(rise[:], shift[:, 1:1 + BINS], shift[:, 0:BINS],
                                             ALU.subtract))
                dve.sem_inc(first_ready, 1)

                dve.wait_ge(cols_done, 3)
                step(nc.vector.tensor_copy(rise_col[0:BINS, :], rise_ps))
                step(nc.vector.tensor_copy(first_col[0][0:BINS, :], first_ps[0]))
                step(nc.vector.tensor_scalar(begun[0][0:BINS, :], iota_u[0:BINS, :],
                                             first_col[0][0:BINS, :], None, ALU.is_ge))
                dve.sem_inc(begun_ready, 1)
                dve.wait_ge(maps_done, 2)
                halves = [slice(n2 * half, (n2 + 1) * half) for n2 in range(2)]
                for n2, part in enumerate(halves):
                    step(nc.vector.tensor_scalar(row[:, part], map_ps[n2][0:1, :], -1.0, None, ALU.add))
                    step(nc.vector.tensor_scalar(less_start[:, part], map_ps[n2], -1.0, -float(BLK),
                                                 ALU.add, ALU.mult))
                dve.sem_inc(map_read, 1)
                step(nc.vector.memset(carried[:], 0.0))
                step(nc.vector.tensor_tensor(carried[:, 1:NS], less_start[:, 1:NS],
                                             less_start[:, 0:NS - 1], ALU.is_equal))
                step(nc.vector.tensor_scalar(carried[:], carried[:], BIG * 2.0**20, -BIG, ALU.mult,
                                             ALU.add))
                step(nc.vector.tensor_copy(bin_of[:], row[:]))
                step(nc.vector.tensor_scalar(row2[:], row[:], float(NBLK), -float(NBLK), ALU.is_ge,
                                             ALU.mult))
                step(nc.vector.tensor_tensor(block_of[:], row[:], row2[:], ALU.add))
                dve.wait_ge(maps_done, 3)
                for n2, part in enumerate(halves):
                    step(nc.vector.scalar_tensor_tensor(row[:, part], iota_u[0:1, part], float(ST),
                                                        map_ps[n2][0:1, :], ALU.mult, ALU.add))
                step(nc.vector.tensor_scalar(window_of[:], row[:], float(2 * E), None, ALU.min))

                rank(key[:, 1, :], 0, NBLK, NBLK, flag, cum, pos[:, 1, :], EP, slot[:, 1, :], slots_done)
                step(nc.vector.memset(slot[:, 0, :], 0))
                falls_in = dve.value_load(unsorted[0:1, 0:1], min_val=0, max_val=E)
                with dve.If(falls_in > 0):
                    rank(key[:, 0, :], 0, 0, NBLK, flag, cum, pos[:, 0, :], EP, slot[:, 0, :], slots_done)
        ctx.close()

    def edges():
        ctx = ExitStack()

        def sb(name, shape, dt):
            return ctx.enter_context(nc.sbuf_tensor(name, shape, dt))

        freq = sb("freq", [EP, 2, TD], F32)
        wb = sb("wb", [EP, 2, TD], F32)
        turns = [sb(f"turns{h}", [EP, CG, 3, TD], F32) for h in range(2)]
        whole_turns = [sb(f"whole_turns{h}", [EP, CG, 3, TD], F32) for h in range(2)]
        rec = [sb(f"rec{h}", [EP, 2, CG, REC], F32) for h in range(2)]
        idx = [sb(f"idx{h}", [EP, 2, CG], I32) for h in range(2)]
        wb_in, freq_ready, part = sem("wb_in"), sem("freq_ready"), sem("turns_part")
        turns_ready, meta_ready, emb_ready = sem("turns_ready"), sem("meta_ready"), sem("emb_ready")
        sent = [[sem(f"sent{d}{h}") for h in range(2)] for d in range(2)]

        def loop(eng, body):
            body(0)
            with eng.Fori(1, NG // 2) as it:
                body(it)

        def all_sent(eng, d):
            for h in range(2):
                eng.wait_ge(sent[d][h], 16 * CG * (NG // 2))

        with nc.Block() as block:
            @block.sync
            def _(sp):
                sp.dma_start(wb[:, 0, :], w_time.partition_broadcast(EP)).then_inc(wb_in, 16)
                sp.dma_start(wb[:, 1, :], b_time.partition_broadcast(EP)).then_inc(wb_in, 16)

                by_partition = records[0:E, :].rearrange("(p c) r -> p c r", p=EP)

                def body(it):
                    for h in range(2):
                        i = 2 * it + h
                        wait_apart(sp, passed[0], (emb_ready, i + 1))
                        wait_apart(sp, passed[0], (meta_ready, 2 * i + 2))
                        sp.dma_start(by_partition[:, at(i * CG, CG), :], rec[h][:, 0, :, :]
                                     ).then_inc(sent[0][h], 16)
                        sp.sem_inc(sent[0][h], 16 * (CG - 1))
                falls_in = sp.value_load(unsorted[0:1, 0:1], min_val=0, max_val=E)
                with sp.If(falls_in < 1):
                    loop(sp, body)
                all_sent(sp, 0)

            @block.vector
            def _(dve):
                dve.wait_ge(wb_in, 32)
                nc.vector.tensor_scalar(freq[:, 0, :], wb[:, 0, :], float(1 / (2 * np.pi)), None,
                                        ALU.mult).then_inc(freq_ready, 1)
                nc.vector.tensor_scalar(freq[:, 1, :], wb[:, 1, :], float(1 / (2 * np.pi)), 0.25,
                                        ALU.mult, ALU.add).then_inc(freq_ready, 1)
                dve.wait_ge(freq_ready, 2)

                def body(it):
                    for h in range(2):
                        i = 2 * it + h
                        c0 = i * CG
                        shape = [EP, CG, 3, TD]
                        wait(dve, emb_ready, i - 1)
                        nc.vector.tensor_tensor(
                            turns[h][:], log_time[:, at(c0, CG), :].unsqueeze(3).broadcast_to(shape),
                            freq[:, 0:1, :].unsqueeze(1).broadcast_to(shape), ALU.mult).then_inc(part, 1)
                        dve.wait_ge(part, 3 * i + 1)
                        nc.vector.tensor_tensor(
                            turns[h][:], turns[h][:],
                            freq[:, 1:2, :].unsqueeze(1).broadcast_to(shape), ALU.add).then_inc(part, 1)
                        dve.wait_ge(part, 3 * i + 2)
                        nc.vector.tensor_scalar(whole_turns[h][:], turns[h][:], ROUND, -ROUND, ALU.add,
                                                ALU.add).then_inc(part, 1)
                        dve.wait_ge(part, 3 * i + 3)
                        nc.vector.tensor_tensor(turns[h][:], turns[h][:], whole_turns[h][:],
                                                ALU.subtract).then_inc(turns_ready, 1)
                        for d in range(2):
                            wait(dve, sent[d][h], 16 * CG * it)
                        nc.vector.tensor_copy(rec[h][:, :, :, 0:2].bitcast(I32),
                                              meta[:, :, at(c0, CG), :]).then_inc(meta_ready, 1)
                        nc.vector.tensor_copy(idx[h][:], slot[:, :, at(c0, CG)]).then_inc(meta_ready, 1)
                loop(dve, body)

            @block.scalar
            def _(act):
                def body(it):
                    for h in range(2):
                        i = 2 * it + h
                        act.wait_ge(turns_ready, i + 1)
                        for d in range(2):
                            wait(act, sent[d][h], 16 * CG * it)
                        emb = rec[h][:, :, :, 2:REC].rearrange("p d c (t w) -> p d c t w", w=TD)
                        nc.scalar.activation(emb[:, 0, :, :, :], turns[h][:], ACT.Sin, scale=TWO_PI)
                        for place, time in enumerate((0, 2, 1)):
                            ins = nc.scalar.activation(emb[:, 1, :, place, :], turns[h][:, :, time, :],
                                                       ACT.Sin, scale=TWO_PI)
                        ins.then_inc(emb_ready, 1)
                loop(act, body)

            @block.gpsimd
            def _(pool):
                def scatter(directions):
                    def body(it):
                        for h in range(2):
                            i = 2 * it + h
                            wait_apart(pool, passed[1], (emb_ready, i + 1), (meta_ready, 2 * i + 2))
                            for c in range(CG):
                                for d in directions:
                                    nc.gpsimd.indirect_dma_start(
                                        records, bass.IndirectOffsetOnAxis(idx[h][:, d, c:c + 1], 0),
                                        rec[h][:, d, c, :], None).then_inc(sent[d][h], 16)
                    return body

                falls_in = pool.value_load(unsorted[0:1, 0:1], min_val=0, max_val=E)
                with pool.If(falls_in > 0):
                    loop(pool, scatter((0, 1)))
                with pool.Else():
                    loop(pool, scatter((1,)))
                all_sent(pool, 1)
        ctx.close()

    def attention():
        outer = ExitStack()
        ctx = ExitStack()
        acc = outer.enter_context(nc.sbuf_tensor("acc", [BLK, BINS, RHS], F32))

        def sb(name, shape, dt):
            return ctx.enter_context(nc.sbuf_tensor(name, shape, dt))

        def several(depth, name, shape, dt):
            copies = [sb(f"{name}{n}", shape, dt) for n in range(depth)]
            return [copies[j % depth] for j in range(UN)]

        pick = sb("pick", [P, HEADS, BLK], BF16)
        eight = sb("eight", [P, 2 * HEADS], F32)
        pick_f = sb("pick_f", [P, HEADS], F32)
        less_one = sb("less_one", [P, 1], F32)

        LONG, SHORT, TWO = 8, 4, 2
        rec = several(LONG, "arec", [P, 2, REC], F32)
        kv = several(LONG, "akv", [P, 2, 2 * KW], F32)
        hot = several(LONG, "hot", [P, 2, BLK], F32)
        qblk = several(SHORT, "qblk", [BLK, 3, DK], BF16)
        place = several(SHORT, "place", [P, 2], F32)
        mixed = several(SHORT, "mixed", [P, 2, P], BF16)
        hotT = several(SHORT, "hotT", [BLK, 2, P], BF16)
        qs = several(SHORT, "qs", [P, 2, DK], F32)
        score = several(SHORT, "score", [P, 2, HEADS], F32)
        newtop = several(SHORT, "newtop", [BLK, HEADS], F32)
        topparts = several(SHORT, "topparts", [BLK, 2, HEADS], BF16)
        drop = several(SHORT, "drop", [BLK, HEADS], F32)
        keepf = several(SHORT, "keepf", [BLK, HEADS], F32)
        below = several(SHORT, "below", [P, 2, HEADS], F32)
        rhs = several(SHORT, "rhs", [P, 2, RHS], F32)
        mixedT = several(TWO, "mixedT", [P, 2, P], BF16)
        prod = several(TWO, "prod", [P, 2, KW], F32)
        tmax = several(TWO, "tmax", [BLK, HEADS], F32)

        def bank(name, shape):
            return ctx.enter_context(nc.psum_tensor(name, shape, F32))

        hotT_ps = bank("hotT_ps", [P, 4, P])[0:BLK, 0:2, :]
        q_ps = bank("q_ps", [P, 512])[:, 0:2 * DK].rearrange("p (t d) -> p t d", t=2)
        top_ps = bank("top_ps", [P, 512])[:, 0:2 * HEADS].rearrange("p (t h) -> p t h", t=2)
        mixedT_ps = bank("mixedT_ps", [P, 4, P])[:, 0:2, :]
        wide = bank("wide", [P, HEADS, 2, P])[0:BLK]
        sums_ps = [bank(f"sums_ps{b}", [P, 512])[0:BLK, 0:RHS] for b in range(2)]

        rec_in = [sem(f"rec_in{j}") for j in range(UN)]
        q_in = [sem(f"q_in{j}") for j in range(UN)]
        kv_in = [sem(f"kv_in{j}") for j in range(UN)]
        ready, picked = sem("acc_ready"), sem("picked")
        names = ("placed hot_done hot_cast hotT_mm hotT_sb q_mm q_sb eq_added ek_put e0_put prod_done "
                 "score_done hi_done lo_done mixedT_mm mixedT_sb wide_mm tmax_done newtop_done top_hi top_lo "
                 "drop_done top_mm keepf_done dist_done below_done w_done wv_done sums_mm scaled acc_done")
        S = {n: sem(n) for n in names.split()}

        def four(v):
            return v.rearrange("p t (h d) -> p t h d", h=HEADS)

        def loop(eng, order):
            def turn(it, ends):
                for j in range(UN):
                    for stage, lag in order:
                        it2, j2 = it + (j + lag) // UN, (j + lag) % UN
                        if not ends or 0 <= it2 < NS // UN:
                            stage(it2, j2, UN * it2 + j2)

            turn(-1, True)
            turn(0, True)
            with eng.Fori(1, NS // UN - 1) as it:
                turn(it, False)
            turn(NS // UN - 1, True)
            turn(NS // UN, True)

        with nc.Block() as block:
            @block.sync
            def _(sp):
                def load(it, j, k):
                    wait_apart(sp, passed[0], (S["e0_put"], k - LONG + 1), (S["eq_added"], k - LONG + 1))
                    wait_apart(sp, passed[0], (S["q_mm"], k - SHORT + 1))
                    w = sp.value_load(window_of[0:1, at(k)], min_val=0, max_val=2 * E)
                    sp.dma_start(rec[j][:], records[at(w, ST), :].rearrange("(p t) r -> p t r", t=2)
                                 ).then_inc(rec_in[j], 16)
                    b = sp.value_load(block_of[0:1, at(k)], min_val=0, max_val=NBLK - 1)
                    sp.dma_start(qblk[j][:].rearrange("p a d -> p (a d)"), q_table[at(b * BLK, BLK), :]
                                 ).then_inc(q_in[j], 16)
                loop(sp, [(load, 0)])

            @block.gpsimd
            def _(pool):
                nc.gpsimd.memset(acc[:], 0.0).then_inc(ready, 1)
                nc.gpsimd.memset(newtop[UN - 1][:], 0.0).then_inc(ready, 1)

                def add_eq(it, j, k):
                    pool.wait_ge(S["q_sb"], k + 1)
                    nc.gpsimd.tensor_tensor(qs[j][:, :, KQ:DK], qs[j][:, :, KQ:DK],
                                            rec[j][:, :, 2 + 2 * TD:REC], ALU.add).then_inc(S["eq_added"], 1)

                def products(it, j, k):
                    pool.wait_ge(S["eq_added"], k + 1)
                    pool.wait_ge(S["ek_put"], k + 1)
                    wait(pool, S["score_done"], k - TWO + 1)
                    nc.gpsimd.tensor_tensor(four(prod[j][:]), four(kv[j][:, :, 0:KW]),
                                            qs[j][:].unsqueeze(2).broadcast_to([P, 2, HEADS, DK]),
                                            ALU.mult).then_inc(S["prod_done"], 1)

                def gather(it, j, k):
                    wait_apart(pool, passed[2], (rec_in[j], 16 * it + 16), (S["wv_done"], k - LONG + 1),
                               (S["prod_done"], k - LONG + 1))
                    for t in range(2):
                        nc.gpsimd.indirect_dma_start(
                            kv[j][:, t, :], None, kv_table,
                            bass.IndirectOffsetOnAxis(rec[j][:, t, 1:2].bitcast(I32), 0)
                        ).then_inc(kv_in[j], 16)
                loop(pool, [(add_eq, 2), (products, 2), (gather, 5)])

            @block.tensor
            def _(pe):
                def turn_hot(it, j, k):
                    pe.wait_ge(S["hot_done"], k + 1)
                    wait(pe, S["hotT_sb"], k)
                    for t in range(2):
                        mm = nc.tensor.matmul(hotT_ps[:, t, :], mixed[j][:, t, 0:BLK], ident_b[:],
                                              start=True, stop=True)
                    mm.then_inc(S["hotT_mm"], 1)

                def queries(it, j, k):
                    pe.wait_ge(S["hotT_sb"], k + 1)
                    pe.wait_ge(q_in[j], 16 * it + 16)
                    wait(pe, S["q_sb"], k)
                    for t in range(2):
                        for a in range(3):
                            mm = nc.tensor.matmul(q_ps[:, t, :], hotT[j][:, t, :], qblk[j][:, a, :],
                                                  start=(a == 0), stop=(a == 2), skip_group_check=True)
                    mm.then_inc(S["q_mm"], 1)

                def turn_mixed(it, j, k):
                    pe.wait_ge(S["lo_done"], k + 1)
                    wait(pe, S["mixedT_sb"], k)
                    for t in range(2):
                        mm = nc.tensor.matmul(mixedT_ps[:, t, :], mixed[j][:, t, :], ident_b[:],
                                              start=True, stop=True)
                    mm.then_inc(S["mixedT_mm"], 1)

                def spread_scores(it, j, k):
                    pe.wait_ge(S["mixedT_sb"], k + 1)
                    wait(pe, S["tmax_done"], k)
                    for h in range(HEADS):
                        mm = nc.tensor.matmul(wide[:, h, :, :], pick[:, h, :], mixedT[j][:],
                                              start=True, stop=True, skip_group_check=True)
                    mm.then_inc(S["wide_mm"], 1)

                def tops(it, j, k):
                    pe.wait_ge(S["top_lo"], k + 1)
                    wait(pe, S["dist_done"], k)
                    for t in range(2):
                        for a in range(2):
                            mm = nc.tensor.matmul(top_ps[:, t, :], hotT[j][:, t, :], topparts[j][:, a, :],
                                                  start=(a == 0), stop=(a == 1), skip_group_check=True)
                    mm.then_inc(S["top_mm"], 1)

                def sums(it, j, k):
                    pe.wait_ge(S["wv_done"], k + 1)
                    wait(pe, S["acc_done"], k - 1)
                    for t in range(2):
                        mm = nc.tensor.matmul(sums_ps[j % 2], hot[j][:, t, :], rhs[j][:, t, :],
                                              start=(t == 0), stop=(t == 1))
                    mm.then_inc(S["sums_mm"], 1)

                pe.wait_ge(ready, 2)
                pe.wait_ge(picked, 7)
                loop(pe, [(turn_mixed, 1), (sums, -2), (tops, 0), (turn_hot, 3), (spread_scores, 1),
                          (queries, 3)])

            @block.scalar
            def _(act):
                act.wait_ge(picked, 7)

                def locate(it, j, k):
                    act.wait_ge(rec_in[j], 16 * it + 16)
                    wait(act, S["hot_done"], k - SHORT + 1)
                    nc.scalar.activation(place[j][:], rec[j][:, :, 0].bitcast(I32), ACT.Identity,
                                         bias=less_start[:, at(k)]).then_inc(S["placed"], 1)

                def cast_hot(it, j, k):
                    act.wait_ge(S["hot_done"], k + 1)
                    wait(act, S["sums_mm"], k - LONG + 1)
                    nc.scalar.copy(hot[j][:], mixed[j][:, :, 0:BLK]).then_inc(S["hot_cast"], 1)

                def copy_hotT(it, j, k):
                    act.wait_ge(S["hotT_mm"], k + 1)
                    wait(act, S["top_mm"], k - SHORT + 1)
                    nc.scalar.copy(hotT[j][:], hotT_ps).then_inc(S["hotT_sb"], 1)

                def put_ek(it, j, k):
                    act.wait_ge(kv_in[j], 32 * it + 32)
                    act.wait_ge(rec_in[j], 16 * it + 16)
                    nc.scalar.copy(
                        kv[j][:].rearrange("p t (c k) -> p t c k", c=2)[:, :, :, PROJ:KW],
                        rec[j][:, :, 2 + TD:2 + 2 * TD].unsqueeze(2).broadcast_to([P, 2, 2, TD])
                    ).then_inc(S["ek_put"], 1)

                def put_e0(it, j, k):
                    act.wait_ge(rec_in[j], 16 * it + 16)
                    wait(act, S["sums_mm"], k - SHORT + 1)
                    nc.scalar.copy(rhs[j][:, :, HEADS * HW:RHS], rec[j][:, :, 2:2 + TD]
                                   ).then_inc(S["e0_put"], 1)

                def copy_q(it, j, k):
                    act.wait_ge(S["q_mm"], k + 1)
                    wait(act, S["prod_done"], k - SHORT + 1)
                    nc.scalar.copy(qs[j][:], q_ps).then_inc(S["q_sb"], 1)

                def high_part(it, j, k):
                    act.wait_ge(S["score_done"], k + 1)
                    wait(act, S["mixedT_mm"], k - SHORT + 1)
                    nc.scalar.copy(mixed[j][:, :, BLK:BLK + HEADS], score[j][:]).then_inc(S["hi_done"], 1)

                def copy_mixedT(it, j, k):
                    act.wait_ge(S["mixedT_mm"], k + 1)
                    wait(act, S["wide_mm"], k - TWO + 1)
                    nc.scalar.activation(mixedT[j][:], mixedT_ps, ACT.Identity, bias=less_one[:]
                                         ).then_inc(S["mixedT_sb"], 1)

                def top_high(it, j, k):
                    act.wait_ge(S["newtop_done"], k + 1)
                    wait(act, S["top_mm"], k - SHORT + 1)
                    nc.scalar.copy(topparts[j][:, 0, :], newtop[j][:]).then_inc(S["top_hi"], 1)

                def factor(it, j, k):
                    act.wait_ge(S["drop_done"], k + 1)
                    wait(act, S["scaled"], k - SHORT + 1)
                    nc.scalar.activation(keepf[j][:], drop[j][:], ACT.Exp, scale=SCALE
                                         ).then_inc(S["keepf_done"], 1)

                def weights(it, j, k):
                    act.wait_ge(S["below_done"], k + 1)
                    wait(act, S["sums_mm"], k - SHORT + 1)
                    w = rhs[j][:, :, 0:HEADS * HW].rearrange("p t (h d) -> p t h d", h=HEADS)[:, :, :, DK]
                    nc.scalar.activation(w, below[j][:], ACT.Exp, scale=SCALE).then_inc(S["w_done"], 1)

                loop(act, [(copy_mixedT, 1), (put_e0, 0), (top_high, 0), (factor, 0), (put_ek, 3),
                           (cast_hot, 3), (copy_hotT, 3), (high_part, 2), (weights, 0), (copy_q, 3),
                           (locate, 4)])

            @block.vector
            def _(dve):
                nc.vector.tensor_scalar(eight[:], ident[:, BLK:P], 1.0, None, ALU.mult).then_inc(picked, 1)
                nc.vector.tensor_scalar(less_one[:], iota_col[:], float(BLK), -1.0, ALU.is_lt, ALU.mult
                                        ).then_inc(picked, 1)
                dve.wait_ge(picked, 2)
                nc.vector.tensor_tensor(pick_f[:], eight[:, 0:HEADS], eight[:, HEADS:2 * HEADS], ALU.add
                                        ).then_inc(picked, 1)
                dve.wait_ge(picked, 3)
                for h in range(HEADS):
                    nc.vector.scalar_tensor_tensor(pick[:, h, :], ident[:, 0:BLK], BIG,
                                                   pick_f[:, h:h + 1].broadcast_to([P, BLK]),
                                                   ALU.mult, ALU.add).then_inc(picked, 1)
                dve.wait_ge(ready, 2)
                dve.wait_ge(picked, 7)
                reg = {}

                def load_bin(it, j, k):
                    reg["bin"] = dve.value_load(bin_of[0:1, at(k)], min_val=0, max_val=BINS - 1)

                def one_hot(it, j, k):
                    dve.wait_ge(S["placed"], k + 1)
                    wait(dve, S["mixedT_mm"], k - SHORT + 1)
                    wait(dve, S["hot_cast"], k - SHORT + 1)
                    nc.vector.tensor_tensor(mixed[j][:, :, 0:BLK],
                                            iota_row[:, 0:BLK].unsqueeze(1).broadcast_to([P, 2, BLK]),
                                            place[j][:].unsqueeze(2).broadcast_to([P, 2, BLK]),
                                            ALU.is_equal).then_inc(S["hot_done"], 1)

                def scores(it, j, k):
                    dve.wait_ge(S["prod_done"], k + 1)
                    wait(dve, S["dist_done"], k - SHORT + 1)
                    nc.vector.tensor_reduce(score[j][:], four(prod[j][:]), AX.X, ALU.add
                                            ).then_inc(S["score_done"], 1)

                def low_part(it, j, k):
                    dve.wait_ge(S["hi_done"], k + 1)
                    dve.wait_ge(S["score_done"], k + 1)
                    nc.vector.tensor_tensor(mixed[j][:, :, BLK + HEADS:P], score[j][:],
                                            mixed[j][:, :, BLK:BLK + HEADS], ALU.subtract
                                            ).then_inc(S["lo_done"], 1)

                def tile_max(it, j, k):
                    dve.wait_ge(S["wide_mm"], k + 1)
                    wait(dve, S["newtop_done"], k - TWO + 1)
                    nc.vector.tensor_reduce(tmax[j][:], wide.rearrange("p h t e -> p h (t e)"),
                                            AX.X, ALU.max).then_inc(S["tmax_done"], 1)

                def new_top(it, j, k):
                    dve.wait_ge(S["tmax_done"], k + 1)
                    wait(dve, S["newtop_done"], k)
                    wait(dve, S["top_lo"], k - SHORT + 1)
                    nc.vector.scalar_tensor_tensor(newtop[j][:], newtop[j - 1][:],
                                                   carried[0:BLK, at(k)], tmax[j][:], ALU.min, ALU.max
                                                   ).then_inc(S["newtop_done"], 1)

                def top_drop(it, j, k):
                    dve.wait_ge(S["newtop_done"], k + 1)
                    wait(dve, S["keepf_done"], k - SHORT + 1)
                    nc.vector.scalar_tensor_tensor(drop[j][:], newtop[j - 1][:], carried[0:BLK, at(k)],
                                                   newtop[j][:], ALU.min, ALU.subtract
                                                   ).then_inc(S["drop_done"], 1)

                def top_low(it, j, k):
                    dve.wait_ge(S["top_hi"], k + 1)
                    nc.vector.tensor_tensor(topparts[j][:, 1, :], newtop[j][:], topparts[j][:, 0, :],
                                            ALU.subtract).then_inc(S["top_lo"], 1)

                def distance(it, j, k):
                    dve.wait_ge(S["top_mm"], k + 1)
                    wait(dve, S["w_done"], k - SHORT + 1)
                    nc.vector.tensor_tensor(below[j][:], score[j][:], top_ps, ALU.subtract
                                            ).then_inc(S["dist_done"], 1)

                def clamp(it, j, k):
                    dve.wait_ge(S["dist_done"], k + 1)
                    nc.vector.tensor_scalar(below[j][:], below[j][:], 64.0, None, ALU.min
                                            ).then_inc(S["below_done"], 1)

                def weigh(it, j, k):
                    dve.wait_ge(S["w_done"], k + 1)
                    dve.wait_ge(S["ek_put"], k + 1)
                    dve.wait_ge(S["e0_put"], k + 1)
                    r = rhs[j][:, :, 0:HEADS * HW].rearrange("p t (h d) -> p t h d", h=HEADS)
                    nc.vector.tensor_tensor(r[:, :, :, 0:DK], four(kv[j][:, :, KW:2 * KW]),
                                            r[:, :, :, DK:HW].broadcast_to([P, 2, HEADS, DK]),
                                            ALU.mult).then_inc(S["wv_done"], 1)

                def rescale(it, j, k):
                    dve.wait_ge(S["keepf_done"], k + 1)
                    wait(dve, S["acc_done"], k)
                    mine = acc[:, at(reg["bin"]), 0:HEADS * HW].rearrange("p o (h d) -> p (o h) d", h=HEADS)
                    nc.vector.tensor_tensor(mine, mine, keepf[j][:].unsqueeze(2).broadcast_to([BLK, HEADS, HW]),
                                            ALU.mult).then_inc(S["scaled"], 1)

                def add(it, j, k):
                    dve.wait_ge(S["scaled"], k + 1)
                    dve.wait_ge(S["sums_mm"], k + 1)
                    mine = acc[:, at(reg["bin"]), :].rearrange("p o n -> p (o n)")
                    nc.vector.tensor_tensor(mine, mine, sums_ps[j % 2], ALU.add).then_inc(S["acc_done"], 1)

                loop(dve, [(tile_max, 0), (load_bin, -2), (one_hot, 3), (new_top, 0), (rescale, -2),
                           (top_drop, 0), (top_low, 0), (weigh, -1), (scores, 2), (distance, 0), (add, -2),
                           (clamp, 0), (low_part, 2)])
        ctx.close()

        inv = outer.enter_context(nc.sbuf_tensor("inv", [BLK, BINS, HEADS], F32))
        agg = outer.enter_context(nc.sbuf_tensor("agg", [BLK, NBLK, D], F32))
        fin, agg_ready, agg_stored = sem("normalised"), sem("agg_ready"), sem("agg_stored")
        HB = NBLK // 2
        with nc.Block() as block:
            @block.vector
            def _(dve):
                by_head = acc[:, :, 0:HEADS * HW].rearrange("p b (h d) -> p b h d", h=HEADS)
                nc.vector.tensor_scalar(inv[:], by_head[:, :, :, DK], 1e-16, None, ALU.add).then_inc(fin, 1)
                dve.wait_ge(fin, 1)
                nc.vector.reciprocal(inv[:], inv[:]).then_inc(fin, 1)
                dve.wait_ge(fin, 2)
                nc.vector.tensor_tensor(by_head[:, :, :, 0:DK], by_head[:, :, :, 0:DK],
                                        inv[:].unsqueeze(3).broadcast_to([BLK, BINS, HEADS, DK]),
                                        ALU.mult).then_inc(fin, 1)
                dve.wait_ge(fin, 3)
                for b0, b1 in ((0, HB), (HB, NBLK)):
                    nc.vector.tensor_tensor(
                        agg[:, b0:b1, 0:KW].rearrange("p b (h d) -> p b h d", h=HEADS),
                        by_head[:, b0:b1, :, 0:DK], by_head[:, NBLK + b0:NBLK + b1, :, 0:DK],
                        ALU.add).then_inc(agg_ready, 1)
                    nc.vector.tensor_tensor(agg[:, b0:b1, KW:D], acc[:, b0:b1, HEADS * HW:RHS],
                                            acc[:, NBLK + b0:NBLK + b1, HEADS * HW:RHS],
                                            ALU.add).then_inc(agg_ready, 1)

            @block.sync
            def _(sp):
                agg_rows = agg_table.rearrange("(b p) d -> p b d", p=BLK)
                for n, (b0, b1) in enumerate(((0, HB), (HB, NBLK))):
                    sp.wait_ge(agg_ready, 2 * n + 2)
                    sp.dma_start(agg_rows[:, b0:b1, :], agg[:, b0:b1, :]).then_inc(agg_stored, 16)
                sp.wait_ge(agg_stored, 32)
        outer.close()

    def output():
        ctx = ExitStack()
        G = 4

        def several(many, name, shape, dt):
            return [ctx.enter_context(nc.sbuf_tensor(f"{name}{h}", shape, dt)) for h in range(many)]

        def banks(many, name):
            return [ctx.enter_context(nc.psum_tensor(f"{name}{h}", [P, 512], F32)) for h in range(many)]

        agg = several(G, "oagg", [P, D], F32)
        xg = several(G, "oxg", [P, D], F32)
        aggT = several(G, "aggT", [P, KC, P], F32)
        wa = several(2, "wa", [P, 2 * KC, D], F32)
        bias = several(2, "obias", [1, D], F32)
        gb = several(G, "gb", [P, 2, D], F32)
        y = several(G, "y", [P, D], F32)
        z = several(G, "z", [P, D], F32)
        res = several(G, "res", [P, D], F32)
        stats = several(G, "stats", [P, 6], F32)
        moments = several(G, "moments", [P, 2], F32)
        root = several(G, "root", [P, 1], F32)
        eps = ctx.enter_context(nc.sbuf_tensor("eps", [P, 1], F32))
        aggT_ps = banks(G, "aggT_ps")
        y_banks = banks(2, "y_ps")
        y_ps = [y_banks[g // 2][:, (g % 2) * D:(g % 2 + 1) * D] for g in range(G)]

        wa_in = [sem("wa_in0"), sem("wa_in1")]
        gb_in = [sem(f"gb_in{g}") for g in range(G)]
        agg_in = [sem(f"oagg_in{g}") for g in range(G)]
        xg_in = [sem(f"oxg_in{g}") for g in range(G)]
        stored = [sem(f"out_stored{g}") for g in range(G)]
        turned, turned_sb, y_mm = sem("agg_turned"), sem("agg_turned_sb"), sem("y_mm")
        y_read, gb_read, x_read = sem("y_read"), sem("gb_read"), sem("x_read")
        var_ready, root_ready, norm, res_ready = sem("var_ready"), sem("root_ready"), sem("norm"), sem("res_ready")
        eps_set = sem("eps_set")
        GROUPS = NT // G

        with nc.Block() as block:
            @block.sync
            def _(sp):
                def body(it):
                    types = []
                    for g in range(G):
                        i = G * it + g
                        h = g % 2
                        wait_apart(sp, passed[0], (y_mm, i - 1))
                        t = sp.value_load(type_of[0:1, at(i)], min_val=0, max_val=T - 1)
                        types.append(t)
                        sp.dma_start(wa[h][:], Wa[at(t)].rearrange("o (c k) n -> k (o c) n", k=P)
                                     ).then_inc(wa_in[h], 16)
                        sp.dma_start(bias[h][:], ba[at(t), :]).then_inc(wa_in[h], 16)
                    for g, t in enumerate(types):
                        wait_apart(sp, passed[0], (gb_read, G * it + g - G + 1))
                        for c, b in enumerate((gamma, beta)):
                            sp.dma_start(gb[g][:, c, :],
                                         b[at(t), :].rearrange("o n -> (o n)").partition_broadcast(P)
                                         ).then_inc(gb_in[g], 16)
                body(0)
                with sp.Fori(1, GROUPS) as it:
                    body(it)

            @block.gpsimd
            def _(pool):
                nc.gpsimd.memset(eps[:], LN_EPS).then_inc(eps_set, 1)

                def gather(tile_, table, i, in_):
                    nc.gpsimd.indirect_dma_start(
                        tile_[i % G][:], None, table,
                        bass.IndirectOffsetOnAxis(node_ids[:, i, 1:2], 0)).then_inc(in_[i % G], 16)

                for i in range(G):
                    gather(agg, agg_table, i, agg_in)
                for i in range(G):
                    gather(xg, x, i, xg_in)
                for it in range(GROUPS):
                    for i in range(G * it, G * it + G):
                        if it + 1 < GROUPS:
                            pool.wait_ge(turned, i + 1)
                            gather(agg, agg_table, i + G, agg_in)
                    for i in range(G * it, G * it + G):
                        if it + 1 < GROUPS:
                            pool.wait_ge(x_read, i + 1)
                            gather(xg, x, i + G, xg_in)
                    for i in range(G * it, G * it + G):
                        pool.wait_ge(res_ready, i + 1)
                        nc.gpsimd.indirect_dma_start(
                            out, bass.IndirectOffsetOnAxis(node_ids[:, i, 0:1], 0), res[i % G][:], None,
                            bounds_check=N - 1, oob_is_err=False).then_inc(stored[i % G], 16)
                for g in range(G):
                    pool.wait_ge(stored[g], 16 * GROUPS)

            @block.tensor
            def _(pe):
                def turn(it):
                    for g in range(G):
                        i = G * it + g
                        pe.wait_ge(agg_in[g], 16 * it + 16)
                        wait(pe, turned_sb, i - G + 1)
                        for c in range(KC):
                            mm = nc.tensor.transpose(aggT_ps[g][:, c * P:(c + 1) * P],
                                                     agg[g][:, c * P:(c + 1) * P], ident[:])
                        mm.then_inc(turned, 1)

                def project(it):
                    for g in range(G):
                        i = G * it + g
                        h = g % 2
                        pe.wait_ge(wa_in[h], 32 * (2 * it + g // 2) + 32)
                        wait(pe, y_read, G * it - 2 + 2 * (g // 2))
                        nc.tensor.matmul(y_ps[g], ones[0:1, :], bias[h][:], start=True, stop=False)
                        pe.wait_ge(turned_sb, i + 1)
                        for c in range(2 * KC):
                            mm = nc.tensor.matmul(y_ps[g], aggT[g][:, c % KC, :], wa[h][:, c, :],
                                                  start=False, stop=(c == 2 * KC - 1))
                        mm.then_inc(y_mm, 1)

                turn(0)
                project(0)
                with pe.Fori(1, GROUPS) as it:
                    turn(it)
                    project(it)

            @block.scalar
            def _(act):
                act.wait_ge(eps_set, 1)

                def copy(it):
                    for g in range(G):
                        i = G * it + g
                        act.wait_ge(turned, i + 1)
                        wait(act, y_mm, i - G + 1)
                        nc.scalar.copy(aggT[g][:],
                                       aggT_ps[g][:, 0:KC * P].rearrange("p (c k) -> p c k", c=KC)
                                       ).then_inc(turned_sb, 1)

                def roots(it, n):
                    for g in range(G):
                        act.wait_ge(var_ready, 2 * G * it + G * n + g + 1)
                        nc.scalar.activation(root[g][:], moments[g][:, 1:2], ACT.Sqrt,
                                             bias=eps[:]).then_inc(root_ready, 1)

                copy(0)
                roots(0, 0)
                with act.Fori(1, GROUPS) as it:
                    copy(it)
                    roots(it - 1, 1)
                    roots(it, 0)
                roots(GROUPS - 1, 1)

            @block.vector
            def _(dve):
                STEPS = 9 * G

                def body(it):
                    done = [0]

                    def step(*made):
                        for m in made:
                            m.then_inc(norm, 1)
                        done[0] += len(made)

                    def passed_all():
                        wait_apart(dve, passed[3], (norm, STEPS * it + done[0]))

                    def mean_and_root(a, n):
                        passed_all()
                        step(*[nc.vector.bn_stats(stats[g][:], a[g][:]) for g in range(G)])
                        passed_all()
                        for g in range(G):
                            nc.vector.bn_aggr(moments[g][:], stats[g][:]).then_inc(var_ready, 1)
                        for g in range(G):
                            dve.wait_ge(root_ready, 2 * G * it + G * n + g + 1)
                            step(nc.vector.reciprocal(root[g][:], root[g][:]))
                        passed_all()

                    def normalise(a, into, g):
                        return nc.vector.tensor_scalar(into[g][:], a[g][:], moments[g][:, 0:1],
                                                       root[g][:, 0:1], ALU.subtract, ALU.mult)

                    wait(dve, res_ready, G * it)
                    for g in range(G):
                        dve.wait_ge(y_mm, G * it + 2 * (g // 2) + 2)
                        dve.wait_ge(xg_in[g], 16 * it + 16)
                        nc.vector.tensor_tensor(y[g][:], y_ps[g], xg[g][:], ALU.add).then_inc(y_read, 1)
                    wait_apart(dve, passed[3], (y_read, G * it + G))
                    mean_and_root(y, 0)
                    step(*[normalise(y, z, g) for g in range(G)])
                    for g in range(G):
                        dve.wait_ge(gb_in[g], 32 * it + 32)
                    passed_all()
                    step(*[nc.vector.tensor_tensor(z[g][:], z[g][:], gb[g][:, 0, :], ALU.mult)
                           for g in range(G)])
                    passed_all()
                    for g in range(G):
                        nc.vector.tensor_tensor(z[g][:], z[g][:], gb[g][:, 1, :], ALU.add
                                                ).then_inc(gb_read, 1)
                    wait_apart(dve, passed[3], (gb_read, G * it + G))
                    for g in range(G):
                        nc.vector.tensor_tensor(y[g][:], z[g][:], xg[g][:], ALU.add).then_inc(x_read, 1)
                    wait_apart(dve, passed[3], (x_read, G * it + G))
                    mean_and_root(y, 1)
                    for g in range(G):
                        wait(dve, stored[g], 16 * it)
                        normalise(y, res, g).then_inc(res_ready, 1)
                    assert done[0] <= STEPS
                    if done[0] < STEPS:
                        dve.sem_inc(norm, STEPS - done[0])
                body(0)
                with dve.Fori(1, GROUPS) as it:
                    body(it)
        ctx.close()

    prepare()
    edges()
    early.close()
    attention()
    output()
    whole.close()


_INS = ['x', 'src', 'dst', 'edge_attr_5', 'node_type_19', 'L0_gnn_Wk', 'L0_gnn_bk', 'L0_gnn_Wq', 'L0_gnn_bq',
        'L0_gnn_Wv', 'L0_gnn_bv', 'L0_gnn_Wa', 'L0_gnn_ba', 'L0_gnn_gamma', 'L0_gnn_beta', 'L0_gnn_w_time',
        'L0_gnn_b_time']


def kernel(**inputs):
    import numpy as _np
    import concourse.bacc as _bacc
    from concourse import mybir as _mybir
    from concourse.bass_utils import run_bass_kernel_spmd as _run

    nc = _bacc.Bacc("TRN2", target_bir_lowering=False, num_devices=1)
    arrays, args = {}, []
    for name in _INS:
        a = _np.ascontiguousarray(inputs[name])
        arrays[f"in_{name}_dram"] = a
        args.append(nc.dram_tensor(f"in_{name}_dram", a.shape, _mybir.dt.from_np(a.dtype), kind="ExternalInput").ap())
    shape = inputs['x'].shape
    args.append(nc.dram_tensor("out_0_dram", list(shape), _mybir.dt.float32, kind="ExternalOutput").ap())
    gnn_kernel(nc, *args)
    r = _run(nc, [arrays], core_ids=[0])
    return r.results[0]["out_0_dram"]
```
